# Optimizing a Trainium2 kernel written in Bass

```python
import numpy as np
import jax
import jax.numpy as jnp

def _softmax(x, axis=-1):
    return jax.nn.softmax(x, axis=axis)

def _gelu(x):
    return jax.nn.gelu(x, approximate=True)

def _silu(x):
    return jax.nn.silu(x)

def _sigmoid(x):
    return jax.nn.sigmoid(x)

def _layernorm(x, axis=-1, eps=1e-05):
    m = jnp.mean(x, axis=axis, keepdims=True)
    v = jnp.var(x, axis=axis, keepdims=True)
    return (x - m) / jnp.sqrt(v + eps)

def _scatter_add(tgt, idx, src, axis=0):
    return tgt.at[idx].add(src)

def _segment_sum(src, seg, n):
    return jax.ops.segment_sum(src, seg, n)
kernel_name = 'mk_dlrm_tower_d1_rec_r8_aae74c'

def setup_inputs(seed: int=0):
    np.random.seed(seed)
    _w = jnp.asarray

    def _rec_inputs():
        import jax
        import jax.numpy as jnp
        _tk = jax.random.key(seed)
        dense_ctx = jax.random.normal(jax.random.fold_in(_tk, 190), (512, 16), jnp.float32)
        ids = jnp.stack([jax.random.randint(jax.random.fold_in(_tk, 200 + f), (512,), 0, v, jnp.int32) for f, v in enumerate([12500, 12500, 1000, 125000, 12500, 125000, 1000, 1000, 12500, 1000, 1250, 12500, 125000, 125000, 1250, 125000, 1000, 12500, 1250, 125000, 12500, 1250, 125000, 1250, 1250, 1250])], axis=1)
        tbl_0 = 0.05 * jax.random.normal(jax.random.fold_in(_tk, 500 + 0), (12500, 32), jnp.float32)
        tbl_1 = 0.05 * jax.random.normal(jax.random.fold_in(_tk, 500 + 1), (12500, 32), jnp.float32)
        tbl_2 = 0.05 * jax.random.normal(jax.random.fold_in(_tk, 500 + 2), (1000, 32), jnp.float32)
        tbl_3 = 0.05 * jax.random.normal(jax.random.fold_in(_tk, 500 + 3), (125000, 32), jnp.float32)
        tbl_4 = 0.05 * jax.random.normal(jax.random.fold_in(_tk, 500 + 4), (12500, 32), jnp.float32)
        tbl_5 = 0.05 * jax.random.normal(jax.random.fold_in(_tk, 500 + 5), (125000, 32), jnp.float32)
        tbl_6 = 0.05 * jax.random.normal(jax.random.fold_in(_tk, 500 + 6), (1000, 32), jnp.float32)
        tbl_7 = 0.05 * jax.random.normal(jax.random.fold_in(_tk, 500 + 7), (1000, 32), jnp.float32)
        tbl_8 = 0.05 * jax.random.normal(jax.random.fold_in(_tk, 500 + 8), (12500, 32), jnp.float32)
        tbl_9 = 0.05 * jax.random.normal(jax.random.fold_in(_tk, 500 + 9), (1000, 32), jnp.float32)
        tbl_10 = 0.05 * jax.random.normal(jax.random.fold_in(_tk, 500 + 10), (1250, 32), jnp.float32)
        tbl_11 = 0.05 * jax.random.normal(jax.random.fold_in(_tk, 500 + 11), (12500, 32), jnp.float32)
        tbl_12 = 0.05 * jax.random.normal(jax.random.fold_in(_tk, 500 + 12), (125000, 32), jnp.float32)
        tbl_13 = 0.05 * jax.random.normal(jax.random.fold_in(_tk, 500 + 13), (125000, 32), jnp.float32)
        tbl_14 = 0.05 * jax.random.normal(jax.random.fold_in(_tk, 500 + 14), (1250, 32), jnp.float32)
        tbl_15 = 0.05 * jax.random.normal(jax.random.fold_in(_tk, 500 + 15), (125000, 32), jnp.float32)
        tbl_16 = 0.05 * jax.random.normal(jax.random.fold_in(_tk, 500 + 16), (1000, 32), jnp.float32)
        tbl_17 = 0.05 * jax.random.normal(jax.random.fold_in(_tk, 500 + 17), (12500, 32), jnp.float32)
        tbl_18 = 0.05 * jax.random.normal(jax.random.fold_in(_tk, 500 + 18), (1250, 32), jnp.float32)
        tbl_19 = 0.05 * jax.random.normal(jax.random.fold_in(_tk, 500 + 19), (125000, 32), jnp.float32)
        tbl_20 = 0.05 * jax.random.normal(jax.random.fold_in(_tk, 500 + 20), (12500, 32), jnp.float32)
        tbl_21 = 0.05 * jax.random.normal(jax.random.fold_in(_tk, 500 + 21), (1250, 32), jnp.float32)
        tbl_22 = 0.05 * jax.random.normal(jax.random.fold_in(_tk, 500 + 22), (125000, 32), jnp.float32)
        tbl_23 = 0.05 * jax.random.normal(jax.random.fold_in(_tk, 500 + 23), (1250, 32), jnp.float32)
        tbl_24 = 0.05 * jax.random.normal(jax.random.fold_in(_tk, 500 + 24), (1250, 32), jnp.float32)
        tbl_25 = 0.05 * jax.random.normal(jax.random.fold_in(_tk, 500 + 25), (1250, 32), jnp.float32)
        _rk = jax.random.fold_in(_tk, 7)
        W_top1 = 0.0606339 * jax.random.normal(jax.random.fold_in(_tk, 801), (272, 512), jnp.float32)
        W_top2 = 0.0441942 * jax.random.normal(jax.random.fold_in(_tk, 802), (512, 256), jnp.float32)
        W_top3 = 0.0625 * jax.random.normal(jax.random.fold_in(_tk, 803), (256, 1), jnp.float32)
        b_top1 = jnp.zeros((512,), jnp.float32)
        b_top2 = jnp.zeros((256,), jnp.float32)
        return (dense_ctx, ids, tbl_0, tbl_1, tbl_2, tbl_3, tbl_4, tbl_5, tbl_6, tbl_7, tbl_8, tbl_9, tbl_10, tbl_11, tbl_12, tbl_13, tbl_14, tbl_15, tbl_16, tbl_17, tbl_18, tbl_19, tbl_20, tbl_21, tbl_22, tbl_23, tbl_24, tbl_25, W_top1, b_top1, W_top2, b_top2, W_top3)
    dense_ctx, ids, tbl_0, tbl_1, tbl_2, tbl_3, tbl_4, tbl_5, tbl_6, tbl_7, tbl_8, tbl_9, tbl_10, tbl_11, tbl_12, tbl_13, tbl_14, tbl_15, tbl_16, tbl_17, tbl_18, tbl_19, tbl_20, tbl_21, tbl_22, tbl_23, tbl_24, tbl_25, W_top1, b_top1, W_top2, b_top2, W_top3 = _rec_inputs()

    def _L0_rec_setup():
        import jax, jax.numpy as jnp
        import numpy as np
        M_FIELDS = 26
        H1 = 128
        H2 = 128
        BATCH = 256
        EMB_K = 32

        def _cin_layer(x_prev, x0, W, b):
            return jnp.einsum('bik,bjk,hij->bhk', x_prev, x0, W) + b[None, :, None]
        key = jax.random.key(seed)
        k0, k1, k2, k3, k4 = jax.random.split(key, 5)
        inputs = jax.random.normal(k0, (BATCH, M_FIELDS, EMB_K), dtype=jnp.float32)
        W1 = jax.random.normal(k1, (H1, M_FIELDS, M_FIELDS), dtype=jnp.float32) * 0.05
        b1 = jax.random.normal(k2, (H1,), dtype=jnp.float32) * 0.05
        W2 = jax.random.normal(k3, (H2, H1, M_FIELDS), dtype=jnp.float32) * 0.05
        b2 = jax.random.normal(k4, (H2,), dtype=jnp.float32) * 0.05
        return {'inputs': inputs, 'W1': W1, 'b1': b1, 'W2': W2, 'b2': b2}
    _L0_rec_all = _L0_rec_setup()
    _L0_rec_in = {k: v for k, v in _L0_rec_all.items() if k in ('W1', 'b1', 'W2', 'b2')}
    del _L0_rec_all
    return {'dense_ctx': dense_ctx, 'ids': ids, 'tbl_0': tbl_0, 'tbl_1': tbl_1, 'tbl_2': tbl_2, 'tbl_3': tbl_3, 'tbl_4': tbl_4, 'tbl_5': tbl_5, 'tbl_6': tbl_6, 'tbl_7': tbl_7, 'tbl_8': tbl_8, 'tbl_9': tbl_9, 'tbl_10': tbl_10, 'tbl_11': tbl_11, 'tbl_12': tbl_12, 'tbl_13': tbl_13, 'tbl_14': tbl_14, 'tbl_15': tbl_15, 'tbl_16': tbl_16, 'tbl_17': tbl_17, 'tbl_18': tbl_18, 'tbl_19': tbl_19, 'tbl_20': tbl_20, 'tbl_21': tbl_21, 'tbl_22': tbl_22, 'tbl_23': tbl_23, 'tbl_24': tbl_24, 'tbl_25': tbl_25, 'W_top1': W_top1, 'b_top1': b_top1, 'W_top2': W_top2, 'b_top2': b_top2, 'W_top3': W_top3, 'L0_rec_W1': _L0_rec_in['W1'], 'L0_rec_b1': _L0_rec_in['b1'], 'L0_rec_W2': _L0_rec_in['W2'], 'L0_rec_b2': _L0_rec_in['b2']}

def reference(dense_ctx, ids, tbl_0, tbl_1, tbl_2, tbl_3, tbl_4, tbl_5, tbl_6, tbl_7, tbl_8, tbl_9, tbl_10, tbl_11, tbl_12, tbl_13, tbl_14, tbl_15, tbl_16, tbl_17, tbl_18, tbl_19, tbl_20, tbl_21, tbl_22, tbl_23, tbl_24, tbl_25, W_top1, b_top1, W_top2, b_top2, W_top3, L0_rec_W1, L0_rec_b1, L0_rec_W2, L0_rec_b2):
    import jax
    import jax.numpy as jnp

    def _L0_rec_ref(inputs, W1, b1, W2, b2):
        import jax, jax.numpy as jnp
        import numpy as np
        M_FIELDS = 26
        H1 = 128
        H2 = 128
        BATCH = 256
        EMB_K = 32

        def _cin_layer(x_prev, x0, W, b):
            return jnp.einsum('bik,bjk,hij->bhk', x_prev, x0, W) + b[None, :, None]
        x1 = _cin_layer(inputs, inputs, W1, b1)
        x2 = _cin_layer(x1, inputs, W2, b2)
        res = jnp.concatenate([x1, x2], axis=1)
        return jnp.sum(res, axis=-1)
    e = jnp.stack([tbl_0[ids[:, 0]], tbl_1[ids[:, 1]], tbl_2[ids[:, 2]], tbl_3[ids[:, 3]], tbl_4[ids[:, 4]], tbl_5[ids[:, 5]], tbl_6[ids[:, 6]], tbl_7[ids[:, 7]], tbl_8[ids[:, 8]], tbl_9[ids[:, 9]], tbl_10[ids[:, 10]], tbl_11[ids[:, 11]], tbl_12[ids[:, 12]], tbl_13[ids[:, 13]], tbl_14[ids[:, 14]], tbl_15[ids[:, 15]], tbl_16[ids[:, 16]], tbl_17[ids[:, 17]], tbl_18[ids[:, 18]], tbl_19[ids[:, 19]], tbl_20[ids[:, 20]], tbl_21[ids[:, 21]], tbl_22[ids[:, 22]], tbl_23[ids[:, 23]], tbl_24[ids[:, 24]], tbl_25[ids[:, 25]]], axis=1)
    z = _L0_rec_ref(e, L0_rec_W1, L0_rec_b1, L0_rec_W2, L0_rec_b2)
    z = z.reshape(z.shape[0], -1)
    h = jnp.concatenate([z, dense_ctx], axis=1)
    h = jnp.maximum(h @ W_top1 + b_top1, 0.0)
    h = jnp.maximum(h @ W_top2 + b_top2, 0.0)
    y = h @ W_top3
    return y

_drawn_inputs = setup_inputs


def setup_inputs(seed=0):
    import zlib

    import numpy as np

    out = dict(_drawn_inputs(seed))
    spreads = {'b_top1': (0.0, 2.0), 'b_top2': (0.0, 0.8)}
    factors = {'tbl_0': 8.0,
     'tbl_1': 8.0,
     'tbl_2': 8.0,
     'tbl_3': 8.0,
     'tbl_4': 8.0,
     'tbl_5': 8.0,
     'tbl_6': 8.0,
     'tbl_7': 8.0,
     'tbl_8': 8.0,
     'tbl_9': 8.0,
     'tbl_10': 8.0,
     'tbl_11': 8.0,
     'tbl_12': 8.0,
     'tbl_13': 8.0,
     'tbl_14': 8.0,
     'tbl_15': 8.0,
     'tbl_16': 8.0,
     'tbl_17': 8.0,
     'tbl_18': 8.0,
     'tbl_19': 8.0,
     'tbl_20': 8.0,
     'tbl_21': 7.922,
     'tbl_22': 8.0,
     'tbl_23': 8.0,
     'tbl_24': 8.0,
     'tbl_25': 8.0,
     'L0_rec_W1': 8.0,
     'L0_rec_W2': 4.005,
     'dense_ctx': 5.365}
    for name, (base, spread) in spreads.items():
        noise = np.random.default_rng([zlib.crc32(name.encode()), seed]).standard_normal(out[name].shape)
        drawn = base * np.exp(spread * noise) if base else spread * noise
        out[name] = jnp.asarray(drawn.astype(out[name].dtype))
    for name, factor in factors.items():
        out[name] = (out[name] * factor).astype(out[name].dtype)
    return out
```

```python
from contextlib import ExitStack

import concourse.bass as bass
from concourse import mybir

F32 = mybir.dt.float32
I32 = mybir.dt.int32
ALU = mybir.AluOpType
ACT = mybir.ActivationFunctionType

P = 128
EMB = 32
FIELDS = 26
HALF = FIELDS // 2
SHIFTS = HALF // 2 + 1
WRAP = SHIFTS - 1
HPAIR = HALF * SHIFTS
PAIRS = 2 * HPAIR + 1
C1 = PAIRS - P
ONE = FIELDS
JW = FIELDS + 1
H = 128
BATCH = 512
TILES = BATCH // P
QUADS = 4
GROUPS = P // QUADS
GSTEP = 4
STEPS = GROUPS // GSTEP
NSTEP = GSTEP * QUADS

COL_A = P + 96
COL_B = COL_A + HALF + WRAP
PCOLS = COL_B + HALF + WRAP
M1 = 96 + HALF

PARTS = [(0, 13, COL_A), (13, 20, COL_B), (20, 26, COL_B + 7)]

D_CTX = 16
N_TOP1 = 512
N_TOP2 = 256
MT1 = N_TOP1 // P
MT2 = N_TOP2 // P


def dlrm_tower(nc, dense_ctx, ids, tables, W_top1, b_top1, W_top2, b_top2, W_top3, W1, b1, W2, b2, out):
    with ExitStack() as ctx:
        def sb(name, shape, dt=F32):
            return ctx.enter_context(nc.sbuf_tensor(name, shape, dt))

        def sem(name):
            return ctx.enter_context(nc.semaphore(name))

        w1 = sb("w1", [P, FIELDS, FIELDS])
        w2 = sb("w2", [P, H, FIELDS])
        wt1 = sb("wt1", [P, 2, N_TOP1])
        wt1c = sb("wt1c", [D_CTX, N_TOP1])
        wt2 = sb("wt2", [P, MT1, N_TOP2])
        vec = sb("vec", [10, P])
        dctx = sb("dctx", [P, TILES, D_CTX])
        ident = sb("ident", [P, P])
        ones = sb("ones", [P, P])
        vecT = sb("vecT", [P, 10])
        b2x32 = sb("b2x32", [P, 1])
        dctxT = sb("dctxT", [D_CTX, BATCH])
        w2t = sb("w2t", [P, FIELDS, H])
        w1ab = sb("w1ab", [P, HALF, HALF])
        w1s = sb("w1s", [P, PAIRS])
        ct = [sb(f"ct{s}", [P, HALF, HALF, HALF]) for s in range(2)]
        cross = sb("cross", [P, FIELDS, PAIRS])
        v0 = sb("v0", [P, FIELDS, H])
        v1 = sb("v1", [P, HALF, H])
        w1sT0 = sb("w1sT0", [P, H])
        w1sT1 = sb("w1sT1", [64, H])
        wabT = sb("wabT", [P, HALF, H])
        idx = [sb(f"idx{i}", [P, FIELDS], I32) for i in range(2)]
        rows = sb("rows", [P, FIELDS, EMB])
        prod = sb("prod", [P, GROUPS, PCOLS])
        diag = sb("diag", [P, GROUPS, JW, QUADS])
        t0 = sb("t0", [P, JW, P])
        t1 = sb("t1", [P, HALF + 1, P])
        gram = sb("gram", [P, HALF, P])
        z = [sb(f"z{i}", [P, P]) for i in range(2)]
        zc = sb("zc", [D_CTX, P])
        h1 = sb("h1", [P, MT1, P])
        h2 = sb("h2", [P, MT2, P])
        y = sb("y", [1, BATCH])

        bank = [ctx.enter_context(nc.psum_tensor(f"bank{i}", [P, 512], F32)) for i in range(8)]
        MOM = [(bank[0], bank[1]), (bank[2], bank[3])]
        Z1, Z2, L1, L2 = bank[4], bank[5], bank[6], bank[7]
        SETUP_BANKS = 6

        s_w1, s_w2, s_vec, s_ctx, s_wt = (sem(n) for n in ("s_w1", "s_w2", "s_vec", "s_ctx", "s_wt"))
        s_idx = [sem(f"s_idx{i}") for i in range(2)]
        s_got = [sem(f"s_got{i}") for i in range(3)]
        s_ident = sem("s_ident")
        s_pad = sem("s_pad")
        s_dv = sem("s_dv")
        s_w1s = sem("s_w1s")
        s_cross = sem("s_cross")
        s_su = sem("s_su")
        s_sf = sem("s_sf")
        s_turn = [sem(f"s_turn{i}") for i in range(3)]
        s_dup = sem("s_dup")
        s_diag = sem("s_diag")
        s_pa = sem("s_pa")
        s_pb = sem("s_pb")
        s_mom = sem("s_mom")
        s_e1 = sem("s_e1")
        s_e0 = sem("s_e0")
        s_eg = sem("s_eg")
        s_z = sem("s_z")
        s_zs = sem("s_zs")
        s_zc = sem("s_zc")
        s_l1 = sem("s_l1")
        s_h1 = sem("s_h1")
        s_l2 = sem("s_l2")
        s_h2 = sem("s_h2")
        s_l3 = sem("s_l3")
        s_y = sem("s_y")
        s_out = sem("s_out")
        s_go = sem("s_go")

        setup = [("vec", 0, 1), ("ctx", 0, TILES)]
        setup += [("w2t", j, min(4, FIELDS - j)) for j in range(0, FIELDS, 4)]
        setup += [("ctA", x, min(3, HALF - x)) for x in range(0, HALF, 3)]
        setup += [("ctB", x, min(3, HALF - x)) for x in range(0, HALF, 3)]
        setup += [("wabT", x, min(4, HALF - x)) for x in range(0, HALF, 4)]
        setup += [("w1sT", 0, 2)]
        setup += [("v0", j, min(4, FIELDS - j)) for j in range(0, FIELDS, 4)]
        setup += [("v1", j, min(4, FIELDS - j)) for j in range(0, FIELDS, 4)]
        where = {}
        for q, (kind, first, n) in enumerate(setup):
            where[kind, first] = q + 1
        done = {kind: where[kind, first] for kind, first, n in setup}

        block = ctx.enter_context(nc.Block())

        @block.sync
        def _(sp):
            ids_v = ids.rearrange("(t p) f -> t p f", p=P)
            for i in range(2):
                sp.dma_start(idx[i][:], ids_v[i]).then_inc(s_idx[i], 16)
            sp.dma_start(w2[:], W2).then_inc(s_w2, 16)
            sp.dma_start(w1[:], W1).then_inc(s_w1, 16)
            sp.dma_start(wt1[:], W_top1[0:2 * H, :].rearrange("(c p) n -> p c n", p=P)).then_inc(s_wt, 16)
            sp.dma_start(wt1c[:], W_top1[2 * H:2 * H + D_CTX, :]).then_inc(s_wt, 16)
            sp.dma_start(wt2[:], W_top2.rearrange("(c p) n -> p c n", p=P)).then_inc(s_wt, 16)
            for i in range(2):
                for part, (f0, f1, _) in enumerate(PARTS):
                    sp.wait_ge(s_got[part], 16 * (f1 - f0) * (i + 1))
                sp.dma_start(idx[i][:], ids_v[2 + i]).then_inc(s_idx[i], 16)
            sp.wait_ge(s_y, TILES)
            sp.dma_start(out.rearrange("(o b) c -> o (b c)", o=1), y[:]).then_inc(s_out, 16)
            sp.wait_ge(s_out, 16)

        @block.gpsimd
        def _(pool):
            nc.gpsimd.memset(ones[:], 1.0).then_inc(s_ident, 1)
            pool.wait_ge(s_ident, 1)
            nc.gpsimd.affine_select(out=ident[:], in_=ones[:], compare_op=ALU.is_equal, fill=0.0, base=0,
                                    pattern=[[-1, P]], channel_multiplier=1).then_inc(s_ident, 1)
            with nc.gpsimd.Fori(0, TILES // 2) as u:
                for i in range(2):
                    pool.wait_ge(s_idx[i], u * 16 + 16)
                    for part, (f0, f1, _) in enumerate(PARTS):
                        pool.wait_ge(s_turn[part], u * 2 + i + 1)
                        pool.sem_inc(s_go, 1)
                        for f in range(f0, f1):
                            pool.indirect_dma_start(
                                rows[:, f, :], None, tables[f],
                                bass.IndirectOffsetOnAxis(ap=idx[i][:, f:f + 1], axis=0)).then_inc(s_got[part], 16)

        @block.tensor
        def _(pe):
            pe.sem_inc(s_mom, STEPS)
            pe.sem_inc(s_z, 1)
            pe.sem_inc(s_l1, 1)
            pe.wait_ge(s_ident, 2)

            for q, (kind, x0, n) in enumerate(setup):
                ps = bank[q % SETUP_BANKS]
                if q >= SETUP_BANKS:
                    pe.wait_ge(s_sf, q - SETUP_BANKS + 1)
                if kind == "vec":
                    pe.wait_ge(s_vec, 80)
                    mm = nc.tensor.transpose(ps[:, 0:10], vec[:], ident[0:10, 0:10])
                elif kind == "ctx":
                    pe.wait_ge(s_ctx, 16)
                    for i in range(n):
                        mm = nc.tensor.transpose(ps[0:D_CTX, i * P:(i + 1) * P], dctx[:, i, :], ident[:])
                elif kind == "w2t":
                    if x0 == 0:
                        pe.wait_ge(s_w2, 16)
                    for i in range(n):
                        mm = nc.tensor.transpose(ps[:, i * H:(i + 1) * H], w2[:, :, x0 + i], ident[:])
                elif kind in ("ctA", "ctB"):
                    if x0 == 0:
                        pe.wait_ge(s_w1s, 1)
                        pe.wait_ge(s_sf, done["w2t"])
                    lo = 0 if kind == "ctA" else HALF
                    rhs = w1ab[:] if kind == "ctA" else w1ab[:].rearrange("h b a -> h a b")
                    for i in range(n):
                        mm = nc.tensor.matmul(ps[:, i * HALF * HALF:(i + 1) * HALF * HALF], w2t[:, lo + x0 + i, :], rhs,
                                              start=True, stop=True)
                elif kind == "wabT":
                    for i in range(n):
                        mm = nc.tensor.transpose(ps[0:HALF, i * H:(i + 1) * H], w1ab[:, x0 + i, :], ident[:])
                elif kind == "w1sT":
                    pe.wait_ge(s_w1s, 2)
                    nc.tensor.transpose(ps[:, 0:H], w1s[:, 0:P], ident[:])
                    mm = nc.tensor.transpose(ps[0:C1, H:2 * H], w1s[:, P:PAIRS], ident[:])
                elif kind == "v0":
                    if x0 == 0:
                        pe.wait_ge(s_cross, 1)
                    for i in range(n):
                        cols = slice(i * H, (i + 1) * H)
                        nc.tensor.matmul(ps[:, cols], w1s[:, 0:P], w2t[:, x0 + i, :], start=True, stop=False)
                        mm = nc.tensor.matmul(ps[:, cols], cross[:, x0 + i, 0:P], ident[:], start=False, stop=True)
                elif kind == "v1":
                    for i in range(n):
                        cols = slice(i * H, (i + 1) * H)
                        adds = x0 + i < HALF
                        mm = nc.tensor.matmul(ps[0:C1, cols], w1s[:, P:PAIRS], w2t[:, x0 + i, :], start=True, stop=not adds)
                        if adds:
                            mm = nc.tensor.matmul(ps[0:C1, cols], cross[:, x0 + i, P:PAIRS], ident[:],
                                                  start=False, stop=True)
                mm.then_inc(s_su, 1)
            pe.wait_ge(s_sf, len(setup))
            pe.wait_ge(s_pad, 1)
            pe.wait_ge(s_wt, 48)

            with nc.tensor.Fori(0, TILES) as t:
                pe.wait_ge(s_diag, t * 12 + 12)
                pe.wait_ge(s_pa, t + 1)
                for s in range(STEPS):
                    m0, m1 = MOM[s % 2]
                    pe.wait_ge(s_pb, t * STEPS + s + 1)
                    if s >= 2:
                        pe.wait_ge(s_e0, t * STEPS + s - 1)
                        pe.wait_ge(s_eg, t * STEPS + s - 1)
                    for g in range(GSTEP):
                        G = s * GSTEP + g
                        mov = diag[:, G, :, :].rearrange("p j r -> p (j r)")
                        nc.tensor.matmul(m0[:, g * P:g * P + JW * QUADS], prod[:, G, 0:P], mov, start=True, stop=True)
                        mm = nc.tensor.matmul(m1[0:M1, g * P:g * P + JW * QUADS], prod[:, G, P:P + M1], mov,
                                              start=True, stop=True)
                    mm.then_inc(s_mom, 1)
                pe.wait_ge(s_e0, t * STEPS + STEPS)
                for j in range(FIELDS):
                    nc.tensor.matmul(Z2[:, 0:P], v0[:, j, :], t0[:, j, :], start=j == 0, stop=False)
                nc.tensor.matmul(Z1[:, 0:P], w1sT0[:], t0[:, ONE, :], start=True, stop=False)
                for s in range(HALF):
                    nc.tensor.matmul(Z2[:, 0:P], v1[0:64 + C1, s, :], t1[0:64 + C1, s, :], start=False,
                                     stop=s == HALF - 1)
                nc.tensor.matmul(Z1[:, 0:P], w1sT1[0:C1, :], t1[0:C1, HALF, :], start=False, stop=False)
                pe.wait_ge(s_eg, t * STEPS + STEPS)
                for b in range(HALF):
                    mm = nc.tensor.matmul(Z1[:, 0:P], wabT[96:96 + HALF, b, :], gram[96:96 + HALF, b, :],
                                          start=False, stop=b == HALF - 1)
                mm.then_inc(s_z, 1)
                pe.wait_ge(s_zs, t * 2 + 2)
                pe.wait_ge(s_zc, t + 1)
                for m in range(MT1):
                    cols = slice(m * P, (m + 1) * P)
                    nc.tensor.matmul(L1[:, cols], wt1c[:, cols], zc[:], start=True, stop=False)
                    nc.tensor.matmul(L1[:, cols], wt1[:, 0, cols], z[0][:], start=False, stop=False)
                    mm = nc.tensor.matmul(L1[:, cols], wt1[:, 1, cols], z[1][:], start=False, stop=True)
                mm.then_inc(s_l1, 1)
                pe.wait_ge(s_h1, t * MT1 + MT1)
                for m in range(MT2):
                    cols = slice(m * P, (m + 1) * P)
                    for c in range(MT1):
                        mm = nc.tensor.matmul(L2[:, cols], wt2[:, c, cols], h1[:, c, :], start=c == 0, stop=c == MT1 - 1)
                mm.then_inc(s_l2, 1)
                pe.wait_ge(s_h2, t * MT2 + MT2)
                for c in range(MT2):
                    mm = nc.tensor.matmul(L1[0:1, 0:P], vecT[:, 8 + c:9 + c], h2[:, c, :], start=c == 0, stop=c == MT2 - 1)
                mm.then_inc(s_l3, 1)

        @block.scalar
        def _(act):
            act.dma_start(vec[0:1, :], b1.rearrange("(o n) -> o n", o=1)).then_inc(s_vec, 16)
            act.dma_start(vec[1:2, :], b2.rearrange("(o n) -> o n", o=1)).then_inc(s_vec, 16)
            act.dma_start(vec[2:6, :], b_top1.rearrange("(o n) -> o n", n=P)).then_inc(s_vec, 16)
            act.dma_start(vec[6:8, :], b_top2.rearrange("(o n) -> o n", n=P)).then_inc(s_vec, 16)
            act.dma_start(vec[8:10, :], W_top3.rearrange("(o n) c -> o (n c)", n=P)).then_inc(s_vec, 16)
            act.dma_start(dctx[:], dense_ctx.rearrange("(t p) c -> p t c", p=P)).then_inc(s_ctx, 16)
            for q, (kind, x0, n) in enumerate(setup):
                ps = bank[q % SETUP_BANKS]
                act.wait_ge(s_su, q + 1)
                if kind == "vec":
                    ins = nc.scalar.copy(vecT[:], ps[:, 0:10])
                elif kind == "ctx":
                    ins = nc.scalar.copy(dctxT[:], ps[0:D_CTX, 0:BATCH])
                elif kind == "w2t":
                    ins = nc.scalar.copy(w2t[:, x0:x0 + n, :], ps[:, 0:n * H].rearrange("p (j h) -> p j h", h=H))
                elif kind in ("ctA", "ctB"):
                    ins = nc.scalar.copy(ct[kind == "ctB"][:, x0:x0 + n, :, :].rearrange("p x b a -> p (x b a)"),
                                         ps[:, 0:n * HALF * HALF])
                elif kind == "wabT":
                    ins = nc.scalar.copy(wabT[96:96 + HALF, x0:x0 + n, :],
                                         ps[0:HALF, 0:n * H].rearrange("p (j h) -> p j h", h=H))
                elif kind == "w1sT":
                    nc.scalar.copy(w1sT0[:], ps[:, 0:H])
                    ins = nc.scalar.copy(w1sT1[0:C1, :], ps[0:C1, H:2 * H])
                elif kind == "v0":
                    ins = nc.scalar.copy(v0[:, x0:x0 + n, :], ps[:, 0:n * H].rearrange("p (j h) -> p j h", h=H))
                elif kind == "v1":
                    if x0 == 0:
                        act.wait_ge(s_pad, 1)
                    both = ps[0:C1, 0:n * H].rearrange("p (s o h) -> p s o h", o=2, h=H)
                    half = slice(x0 // 2, x0 // 2 + n // 2)
                    nc.scalar.copy(v1[0:C1, half, :], both[:, :, 0, :])
                    ins = nc.scalar.copy(v1[64:64 + C1, half, :], both[:, :, 1, :])
                ins.then_inc(s_sf, 1)

            with nc.scalar.Fori(0, TILES) as t:
                act.wait_ge(s_mom, t * STEPS + STEPS)
                act.wait_ge(s_pad, 1)
                for part, (f0, f1, col) in enumerate(PARTS):
                    act.wait_ge(s_turn[part], t + 2)
                    for r in range(QUADS):
                        q = slice(32 * r, 32 * r + 32)
                        nc.scalar.copy(diag[q, :, f0:f1, r], prod[q, :, col:col + f1 - f0]).then_inc(s_diag, 1)
                for s in range(STEPS):
                    m0, m1 = MOM[s % 2]
                    n = slice(s * NSTEP, (s + 1) * NSTEP)
                    act.wait_ge(s_mom, t * STEPS + STEPS + s + 1)
                    if s == 0:
                        act.wait_ge(s_z, t + 1)

                    def view(m, p, j0, j1, step):
                        return m[0:p, :].rearrange("p (g j r) -> p j g r", g=GSTEP, r=QUADS)[:, j0:j1:step]

                    def dst(x, p0, p, js):
                        return x[p0:p0 + p, js, n].rearrange("p j (g r) -> p j g r", r=QUADS)

                    nc.scalar.copy(dst(t1, 0, C1, slice(0, HALF + 1)), view(m1, C1, 0, JW, 2))
                    nc.scalar.copy(dst(t1, 64, C1, slice(0, HALF)), view(m1, C1, 1, JW, 2)).then_inc(s_e1, 1)
                    nc.scalar.copy(dst(t0, 0, P, slice(0, JW)), view(m0, P, 0, JW, 1)).then_inc(s_e0, 1)
                act.wait_ge(s_l1, t + 2)
                for m in range(MT1):
                    nc.scalar.activation(h1[:, m, :], L1[:, m * P:(m + 1) * P], ACT.Relu,
                                         bias=vecT[:, 2 + m:3 + m]).then_inc(s_h1, 1)
                act.wait_ge(s_l2, t + 1)
                for m in range(MT2):
                    nc.scalar.activation(h2[:, m, :], L2[:, m * P:(m + 1) * P], ACT.Relu,
                                         bias=vecT[:, 6 + m:7 + m]).then_inc(s_h2, 1)

        @block.vector
        def _(dve):
            chain = [0]

            def link(ins):
                chain[0] += 1
                ins.then_inc(s_dv, 1)

            def linked():
                dve.wait_ge(s_dv, chain[0])

            for part in range(3):
                dve.sem_inc(s_turn[part], 1)
            link(nc.vector.memset(prod[:, :, PAIRS:COL_A], 0.0))
            link(nc.vector.memset(prod[:, :, PAIRS - 1], 1.0))
            link(nc.vector.memset(diag[:], 0.0))
            link(nc.vector.memset(t1[32:64, :, :], 0.0))
            link(nc.vector.memset(v1[32:64, :, :], 0.0))
            linked()
            for r in range(QUADS):
                ins = nc.vector.memset(diag[32 * r:32 * r + 32, :, ONE, r], 1.0)
            ins.then_inc(s_pad, 1)

            dve.wait_ge(s_w1, 16)
            nc.vector.tensor_tensor(w1ab[:], w1[:, 0:HALF, HALF:FIELDS].rearrange("h a b -> h b a"),
                                    w1[:, HALF:FIELDS, 0:HALF], ALU.add).then_inc(s_w1s, 1)
            w1f = w1[:].rearrange("h i l -> h (i l)")
            step = FIELDS + 1

            def diagonal(i, l, n):
                a = i * FIELDS + l
                return w1f[:, a:a + (n - 1) * step + 1:step]

            for side in range(2):
                o = side * HALF
                for d in range(SHIFTS):
                    c = side * HPAIR + d * HALF
                    if d == 0:
                        nc.vector.tensor_copy(w1s[:, c:c + HALF], diagonal(o, o, HALF))
                        continue
                    k = HALF - d
                    nc.vector.tensor_tensor(w1s[:, c:c + k], diagonal(o, o + d, k), diagonal(o + d, o, k), ALU.add)
                    nc.vector.tensor_tensor(w1s[:, c + k:c + HALF], diagonal(o + k, o, d), diagonal(o, o + k, d), ALU.add)
            dve.wait_ge(s_sf, where["vec", 0])
            nc.vector.tensor_scalar(b2x32[:], vecT[:, 1:2], float(EMB), None, ALU.mult)
            nc.vector.tensor_copy(w1s[:, PAIRS - 1:PAIRS], vecT[:, 0:1]).then_inc(s_w1s, 1)
            link(nc.vector.memset(cross[:, 0:HALF, 0:HPAIR], 0.0))
            link(nc.vector.memset(cross[:, HALF:FIELDS, HPAIR:P], 0.0))
            link(nc.vector.memset(cross[:, 0:HALF, PAIRS - 1], 0.0))
            for side in range(2):
                dve.wait_ge(s_sf, done["ctB" if side else "ctA"])
                js = slice(HALF, FIELDS) if side == 0 else slice(0, HALF)

                for d in range(SHIFTS):
                    for i0, n, up in ((0, HALF - d, d), (HALF - d, d, d - HALF)):
                        if n == 0:
                            continue
                        c = side * HPAIR + d * HALF + i0
                        dest = cross[:, js, c:c + n]
                        one = skew(ct[side], i0 + up, i0, n)
                        if d == 0:
                            nc.vector.tensor_copy(dest, one)
                        else:
                            ins = nc.vector.tensor_tensor(dest, one, skew(ct[side], i0, i0 + up, n), ALU.add)
            ins.then_inc(s_cross, 1)

            with nc.vector.Fori(0, TILES) as t:
                dve.wait_ge(s_mom, t * STEPS + STEPS)
                for part, (f0, f1, col) in enumerate(PARTS):
                    dve.wait_ge(s_got[part], (t + 1) * (16 * (f1 - f0)))
                    nc.vector.transpose(prod[:, :, col:col + f1 - f0].rearrange("p g f -> p f g"),
                                        rows[:, f0:f1, :]).then_inc(s_turn[part], 1)
                    if part == 0:
                        dve.wait_ge(s_turn[0], t + 2)
                        nc.vector.tensor_copy(prod[:, :, COL_A + HALF:COL_A + HALF + WRAP],
                                              prod[:, :, COL_A:COL_A + WRAP]).then_inc(s_dup, 1)
                        dve.wait_ge(s_dup, t * 2 + 1)
                        products(nc.vector, prod, 0, GROUPS, COL_A, 0).then_inc(s_pa, 1)
                    if part == 1:
                        dve.wait_ge(s_turn[1], t + 2)
                        nc.vector.tensor_copy(prod[:, :, COL_B + HALF:COL_B + HALF + WRAP],
                                              prod[:, :, COL_B:COL_B + WRAP]).then_inc(s_dup, 1)
                dve.wait_ge(s_turn[2], t + 2)
                dve.wait_ge(s_dup, t * 2 + 2)
                for s in range(STEPS + 2):
                    if s < STEPS:
                        products(nc.vector, prod, s * GSTEP, GSTEP, COL_B, HPAIR).then_inc(s_pb, 1)
                    if s >= 2:
                        m1 = MOM[s % 2][1]
                        dve.wait_ge(s_mom, t * STEPS + STEPS + s - 1)
                        dve.wait_ge(s_e1, t * STEPS + s - 1)
                        if s == 2:
                            dve.wait_ge(s_z, t + 1)
                        n = slice((s - 2) * NSTEP, (s - 1) * NSTEP)
                        nc.vector.tensor_copy(
                            gram[96:96 + HALF, :, n].rearrange("p j (g r) -> p j g r", r=QUADS),
                            m1[96:96 + HALF, :].rearrange("p (g j r) -> p j g r", g=GSTEP, r=QUADS)[:, HALF:FIELDS]
                        ).then_inc(s_eg, 1)
                dve.wait_ge(s_l1, t + 1)
                nc.vector.tensor_copy(zc[:].rearrange("p (g r) -> p r g", r=QUADS),
                                      dctxT[:, bass.ds(t * P, P)].rearrange("p (r g) -> p r g", r=QUADS)).then_inc(s_zc, 1)
                dve.wait_ge(s_z, t + 2)
                nc.vector.tensor_copy(z[0][:], Z1[:, 0:P]).then_inc(s_zs, 1)
                nc.vector.tensor_scalar(z[1][:], Z2[:, 0:P], b2x32[:, 0:1], None, ALU.add).then_inc(s_zs, 1)
                dve.wait_ge(s_l3, t + 1)
                nc.vector.tensor_copy(y[0:1, bass.ds(t * P, P)].rearrange("p (r g) -> p r g", r=QUADS),
                                      L1[0:1, 0:P].rearrange("p (g r) -> p r g", r=QUADS)).then_inc(s_y, 1)


def skew(ct, x, a, n):
    return with_dims(ct[:, x, :, a:a + 1], [HALF, HALF], [HALF * HALF + 1, n])


def with_dims(ap, *dims):
    return bass.AP(tensor=ap.tensor, offset=ap.offset, ap=[list(ap.ap[0])] + [list(d) for d in dims])


def products(eng, prod, g0, groups, col, pair0):
    dst = prod[:, g0:g0 + groups, pair0:pair0 + HPAIR].rearrange("p g (d i) -> p g d i", i=HALF)
    start = prod[:, g0:g0 + groups, col:col + HALF]
    left = with_dims(start, [PCOLS, groups], [0, SHIFTS], [1, HALF])
    right = with_dims(start, [PCOLS, groups], [1, SHIFTS], [1, HALF])
    return eng.tensor_tensor(dst, left, right, ALU.mult)


NAMES = (["dense_ctx", "ids"] + [f"tbl_{i}" for i in range(FIELDS)]
         + ["W_top1", "b_top1", "W_top2", "b_top2", "W_top3", "L0_rec_W1", "L0_rec_b1", "L0_rec_W2", "L0_rec_b2"])


def kernel(**inputs):
    import numpy as _np
    import concourse.bacc as _bacc
    from concourse import mybir as _mybir
    from concourse.bass_utils import run_bass_kernel_spmd as _run

    nc = _bacc.Bacc("TRN2", target_bir_lowering=False, num_devices=1)
    arrays, aps = {}, {}
    for name in NAMES:
        a = _np.ascontiguousarray(inputs[name])
        arrays[f"in_{name}_dram"] = a
        aps[name] = nc.dram_tensor(f"in_{name}_dram", a.shape, _mybir.dt.from_np(a.dtype), kind="ExternalInput").ap()
    out = nc.dram_tensor("out_0_dram", (BATCH, 1), _mybir.dt.float32, kind="ExternalOutput").ap()
    dlrm_tower(nc, aps["dense_ctx"], aps["ids"], [aps[f"tbl_{i}"] for i in range(FIELDS)],
               aps["W_top1"], aps["b_top1"], aps["W_top2"], aps["b_top2"], aps["W_top3"],
               aps["L0_rec_W1"], aps["L0_rec_b1"], aps["L0_rec_W2"], aps["L0_rec_b2"], out)
    r = _run(nc, [arrays], core_ids=[0])
    return r.results[0]["out_0_dram"]
```

```python
from contextlib import ExitStack

import concourse.bass as bass
from concourse import mybir

F32 = mybir.dt.float32
I32 = mybir.dt.int32
ALU = mybir.AluOpType
ACT = mybir.ActivationFunctionType

P = 128
EMB = 32
FIELDS = 26
HALF = FIELDS // 2
SHIFTS = HALF // 2 + 1
WRAP = SHIFTS - 1
HPAIR = HALF * SHIFTS
PAIRS = 2 * HPAIR + 1
C1 = PAIRS - P
ONE = FIELDS
JW = FIELDS + 1
H = 128
BATCH = 512
TILES = BATCH // P
QUADS = 4
GROUPS = P // QUADS
GSTEP = 4
STEPS = GROUPS // GSTEP
NSTEP = GSTEP * QUADS

COL_A2 = P + 64
COL_A = P + 96
GB = HALF - HALF // 2
COL_B = COL_A + HALF + WRAP
PCOLS = COL_B + HALF + WRAP
M1 = 96 + HALF

PARTS = [(0, 13, COL_A), (13, 20, COL_B), (20, 26, COL_B + 7)]

WARM = 14
D_CTX = 16
N_TOP1 = 512
N_TOP2 = 256
MT1 = N_TOP1 // P
MT2 = N_TOP2 // P


def dlrm_tower(nc, dense_ctx, ids, tables, W_top1, b_top1, W_top2, b_top2, W_top3, W1, b1, W2, b2, out):
    with ExitStack() as ctx:
        def sb(name, shape, dt=F32):
            return ctx.enter_context(nc.sbuf_tensor(name, shape, dt))

        def sem(name):
            return ctx.enter_context(nc.semaphore(name))

        w1 = sb("w1", [P, FIELDS, FIELDS])
        w2 = sb("w2", [P, H, FIELDS])
        wt1 = sb("wt1", [P, 2, N_TOP1])
        wt1c = sb("wt1c", [D_CTX, N_TOP1])
        wt2 = sb("wt2", [P, MT1, N_TOP2])
        vec = sb("vec", [10, P])
        dctx = sb("dctx", [P, TILES, D_CTX])
        ident = sb("ident", [P, P])
        ones = sb("ones", [P, P])
        vecT = sb("vecT", [P, 10])
        b2x32 = sb("b2x32", [P, 1])
        dctxT = sb("dctxT", [D_CTX, BATCH])
        w2t = sb("w2t", [P, FIELDS, H])
        w1ab = sb("w1ab", [P, HALF, HALF])
        w1s = sb("w1s", [P, PAIRS])
        ct = [sb(f"ct{s}", [P, HALF, HALF, HALF]) for s in range(2)]
        folded = sb("folded", [P, FIELDS, PAIRS])
        v0 = sb("v0", [P, FIELDS, H])
        v1 = sb("v1", [P, HALF, H])
        w1sT0 = sb("w1sT0", [P, H])
        w1c = sb("w1c", [P, GB, H])
        idx = [sb(f"idx{i}", [P, FIELDS], I32) for i in range(2)]
        rows = sb("rows", [P, FIELDS, EMB])
        prod = sb("prod", [P, GROUPS, PCOLS])
        diag = sb("diag", [P, GROUPS, JW, QUADS])
        t0 = sb("t0", [P, JW, P])
        t1 = sb("t1", [P, HALF + GB, P])
        z = [sb(f"z{i}", [P, P]) for i in range(2)]
        h1 = sb("h1", [P, MT1, P])
        h2 = sb("h2", [P, MT2, P])
        y = sb("y", [1, BATCH])

        bank = [ctx.enter_context(nc.psum_tensor(f"bank{i}", [P, 512], F32)) for i in range(8)]
        MOM = [(bank[0], bank[1]), (bank[2], bank[3])]
        Z1, Z2, L1, L2 = bank[4], bank[5], bank[6], bank[7]
        SETUP_BANKS = 6

        s_w1, s_w2, s_vec, s_ctx, s_wt = (sem(n) for n in ("s_w1", "s_w2", "s_vec", "s_ctx", "s_wt"))
        s_idx = [sem(f"s_idx{i}") for i in range(2)]
        s_got = [sem(f"s_got{i}") for i in range(3)]
        s_ident = sem("s_ident")
        s_pad = sem("s_pad")
        s_dv = sem("s_dv")
        s_w1s = sem("s_w1s")
        s_cross = sem("s_cross")
        s_su = sem("s_su")
        s_sf = sem("s_sf")
        s_turn = [sem(f"s_turn{i}") for i in range(3)]
        s_dup = sem("s_dup")
        s_diag = sem("s_diag")
        s_pa = sem("s_pa")
        s_pb = sem("s_pb")
        s_mom = sem("s_mom")
        s_e1 = sem("s_e1")
        s_e0 = sem("s_e0")
        s_eg = sem("s_eg")
        s_z = sem("s_z")
        s_zs = sem("s_zs")
        s_l1 = sem("s_l1")
        s_h1 = sem("s_h1")
        s_l2 = sem("s_l2")
        s_h2 = sem("s_h2")
        s_l3 = sem("s_l3")
        s_y = sem("s_y")
        s_out = sem("s_out")
        s_go = sem("s_go")

        setup = [("vec", 0, 1)]
        setup += [("w2t", j, min(4, FIELDS - j)) for j in range(0, FIELDS, 4)]
        setup += [("fold", j, 2) for j in range(0, FIELDS, 2)]
        setup += [("ctA", x, min(3, HALF - x)) for x in range(0, HALF, 3)]
        setup += [("ctB", x, min(3, HALF - x)) for x in range(0, HALF, 3)]
        setup += [("ctx", 0, TILES)]
        setup += [("wabT", x, min(4, HALF - x)) for x in range(0, HALF, 4)]
        setup += [("w1sT", 0, 2)]
        setup += [("v0", j, min(4, FIELDS - j)) for j in (16, 20, 24, 12, 0, 4, 8)]
        setup += [("v1", j, min(4, FIELDS - j)) for j in range(0, FIELDS, 4)]
        where = {}
        for q, (kind, first, n) in enumerate(setup):
            where[kind, first] = q + 1
        done = {kind: where[kind, first] for kind, first, n in setup}

        block = ctx.enter_context(nc.Block())

        @block.sync
        def _(sp):
            ids_v = ids.rearrange("(t p) f -> t p f", p=P)
            for i in range(2):
                sp.dma_start(idx[i][:], ids_v[i]).then_inc(s_idx[i], 16)
            sp.dma_start(w1[:], W1).then_inc(s_w1, 16)
            sp.dma_start(w2[:, 0:H // 2, :], W2[:, 0:H // 2, :]).then_inc(s_w2, 16)
            sp.dma_start(wt1[:], W_top1[0:2 * H, :].rearrange("(c p) n -> p c n", p=P)).then_inc(s_wt, 16)
            sp.dma_start(wt1c[:], W_top1[2 * H:2 * H + D_CTX, :]).then_inc(s_wt, 16)
            sp.dma_start(wt2[:], W_top2.rearrange("(c p) n -> p c n", p=P)).then_inc(s_wt, 16)
            for i in range(2):
                for part, (f0, f1, _) in enumerate(PARTS):
                    sp.wait_ge(s_got[part], 16 * (f1 - f0) * (i + 1))
                sp.dma_start(idx[i][:], ids_v[2 + i]).then_inc(s_idx[i], 16)
            sp.wait_ge(s_y, TILES)
            sp.dma_start(out.rearrange("(o b) c -> o (b c)", o=1), y[:]).then_inc(s_out, 16)
            sp.wait_ge(s_out, 16)

        @block.gpsimd
        def _(pool):
            nc.gpsimd.memset(ones[:], 1.0).then_inc(s_ident, 1)
            pool.wait_ge(s_ident, 1)
            nc.gpsimd.affine_select(out=ident[:], in_=ones[:], compare_op=ALU.is_equal, fill=0.0, base=0,
                                    pattern=[[-1, P]], channel_multiplier=1).then_inc(s_ident, 1)
            with nc.gpsimd.Fori(0, TILES // 2) as u:
                for i in range(2):
                    pool.wait_ge(s_idx[i], u * 16 + 16)
                    for part, (f0, f1, _) in enumerate(PARTS):
                        pool.wait_ge(s_turn[part], u * 2 + i + 1)
                        pool.sem_inc(s_go, 1)
                        for f in range(f0, f1):
                            pool.indirect_dma_start(
                                rows[:, f, :], None, tables[f],
                                bass.IndirectOffsetOnAxis(ap=idx[i][:, f:f + 1], axis=0)).then_inc(s_got[part], 16)

        @block.tensor
        def _(pe):
            pe.sem_inc(s_mom, STEPS)
            pe.sem_inc(s_z, 1)
            pe.wait_ge(s_ident, 2)

            for _ in range(WARM):
                nc.tensor.matmul(L2[:, 0:P], ident[:], ident[:], start=True, stop=True)
            for q, (kind, x0, n) in enumerate(setup):
                ps = bank[q % SETUP_BANKS]
                if q >= SETUP_BANKS:
                    pe.wait_ge(s_sf, q - SETUP_BANKS + 1)
                if kind == "vec":
                    pe.wait_ge(s_vec, 80)
                    mm = nc.tensor.transpose(ps[:, 0:10], vec[:], ident[0:10, 0:10])
                elif kind == "ctx":
                    pe.wait_ge(s_ctx, 16)
                    for i in range(n):
                        mm = nc.tensor.transpose(ps[0:D_CTX, i * P:(i + 1) * P], dctx[:, i, :], ident[:])
                elif kind == "w2t":
                    if x0 == 0:
                        pe.wait_ge(s_w2, 32)
                    for i in range(n):
                        mm = nc.tensor.transpose(ps[:, i * H:(i + 1) * H], w2[:, :, x0 + i], ident[:])
                elif kind == "fold":
                    if x0 == 0:
                        pe.wait_ge(s_w1s, 2)
                        pe.wait_ge(s_sf, done["w2t"])
                    for i in range(n):
                        mm = nc.tensor.matmul(ps[:, i * PAIRS:(i + 1) * PAIRS], w2t[:, x0 + i, :], w1s[:],
                                              start=True, stop=True)
                elif kind in ("ctA", "ctB"):
                    lo = 0 if kind == "ctA" else HALF
                    rhs = w1ab[:] if kind == "ctA" else w1ab[:].rearrange("h b a -> h a b")
                    for i in range(n):
                        mm = nc.tensor.matmul(ps[:, i * HALF * HALF:(i + 1) * HALF * HALF], w2t[:, lo + x0 + i, :], rhs,
                                              start=True, stop=True)
                elif kind == "wabT":
                    for i in range(n):
                        mm = nc.tensor.transpose(ps[0:HALF, i * H:(i + 1) * H], w1ab[:, x0 + i, :], ident[:])
                elif kind == "w1sT":
                    nc.tensor.transpose(ps[:, 0:H], w1s[:, 0:P], ident[:])
                    mm = nc.tensor.transpose(ps[0:C1, H:2 * H], w1s[:, P:PAIRS], ident[:])
                elif kind == "v0":
                    pe.wait_ge(s_cross, 1 if x0 >= HALF else 2)
                    for i in range(n):
                        mm = nc.tensor.transpose(ps[:, i * H:(i + 1) * H], folded[:, x0 + i, 0:P], ident[:])
                elif kind == "v1":
                    for i in range(n):
                        mm = nc.tensor.transpose(ps[0:C1, i * H:(i + 1) * H], folded[:, x0 + i, P:PAIRS], ident[:])
                mm.then_inc(s_su, 1)
            pe.wait_ge(s_sf, len(setup))
            pe.wait_ge(s_pad, 1)
            pe.wait_ge(s_wt, 48)

            def moments(t):
                pe.wait_ge(s_diag, t * 12 + 12)
                pe.wait_ge(s_pa, t + 1)
                for s in range(STEPS):
                    m0, m1 = MOM[s % 2]
                    pe.wait_ge(s_pb, t * STEPS + s + 1)
                    if s >= 2:
                        pe.wait_ge(s_e0, t * STEPS + s - 1)
                        pe.wait_ge(s_eg, t * STEPS + s - 1)
                    for g in range(GSTEP):
                        G = s * GSTEP + g
                        mov = diag[:, G, :, :].rearrange("p j r -> p (j r)")
                        nc.tensor.matmul(m0[:, g * P:g * P + JW * QUADS], prod[:, G, 0:P], mov, start=True, stop=True)
                        mm = nc.tensor.matmul(m1[0:M1, g * P:g * P + JW * QUADS], prod[:, G, P:P + M1], mov,
                                              start=True, stop=True)
                    mm.then_inc(s_mom, 1)

            def z2_first(t):
                pe.wait_ge(s_e0, t * STEPS + STEPS)
                for j in range(FIELDS):
                    nc.tensor.matmul(Z2[:, 0:P], v0[:, j, :], t0[:, j, :], start=j == 0, stop=False)

            def z2_rest_z1(t):
                for s in range(HALF):
                    nc.tensor.matmul(Z2[:, 0:P], v1[0:64 + C1, s, :], t1[0:64 + C1, s, :], start=False,
                                     stop=s == HALF - 1)
                nc.tensor.matmul(Z1[:, 0:P], w1sT0[:], t0[:, ONE, :], start=True, stop=False)
                pe.wait_ge(s_eg, t * STEPS + STEPS)
                for b in range(GB):
                    k = slice(0 if b == 0 else 64, M1)
                    mm = nc.tensor.matmul(Z1[:, 0:P], w1c[k, b, :], t1[k, HALF + b, :], start=False, stop=b == GB - 1)
                mm.then_inc(s_z, 1)

            def mlp1(t):
                pe.wait_ge(s_zs, t * 2 + 2)
                for m in range(MT1):
                    cols = slice(m * P, (m + 1) * P)
                    nc.tensor.matmul(L1[:, cols], wt1c[:, cols], dctxT[:, bass.ds(t * P, P)], start=True, stop=False)
                    nc.tensor.matmul(L1[:, cols], wt1[:, 0, cols], z[0][:], start=False, stop=False)
                    mm = nc.tensor.matmul(L1[:, cols], wt1[:, 1, cols], z[1][:], start=False, stop=True)
                mm.then_inc(s_l1, 1)

            def mlp2(t):
                pe.wait_ge(s_h1, t * MT1 + MT1)
                for m in range(MT2):
                    cols = slice(m * P, (m + 1) * P)
                    for c in range(MT1):
                        mm = nc.tensor.matmul(L2[:, cols], wt2[:, c, cols], h1[:, c, :], start=c == 0, stop=c == MT1 - 1)
                mm.then_inc(s_l2, 1)

            def mlp3(t):
                pe.wait_ge(s_h2, t * MT2 + MT2)
                for c in range(MT2):
                    mm = nc.tensor.matmul(L1[0:1, 0:P], vecT[:, 8 + c:9 + c], h2[:, c, :], start=c == 0, stop=c == MT2 - 1)
                mm.then_inc(s_l3, 1)

            moments(0)
            z2_first(0)
            z2_rest_z1(0)
            with nc.tensor.Fori(1, TILES) as t:
                moments(t)
                mlp1(t - 1)
                z2_first(t)
                mlp2(t - 1)
                z2_rest_z1(t)
                mlp3(t - 1)
            mlp1(TILES - 1)
            mlp2(TILES - 1)
            mlp3(TILES - 1)

        @block.scalar
        def _(act):
            act.dma_start(w2[:, H // 2:H, :], W2[:, H // 2:H, :]).then_inc(s_w2, 16)
            act.dma_start(vec[0:1, :], b1.rearrange("(o n) -> o n", o=1)).then_inc(s_vec, 16)
            act.dma_start(vec[1:2, :], b2.rearrange("(o n) -> o n", o=1)).then_inc(s_vec, 16)
            act.dma_start(vec[2:6, :], b_top1.rearrange("(o n) -> o n", n=P)).then_inc(s_vec, 16)
            act.dma_start(vec[6:8, :], b_top2.rearrange("(o n) -> o n", n=P)).then_inc(s_vec, 16)
            act.dma_start(vec[8:10, :], W_top3.rearrange("(o n) c -> o (n c)", n=P)).then_inc(s_vec, 16)
            act.dma_start(dctx[:], dense_ctx.rearrange("(t p) c -> p t c", p=P)).then_inc(s_ctx, 16)
            for q, (kind, x0, n) in enumerate(setup):
                ps = bank[q % SETUP_BANKS]
                act.wait_ge(s_su, q + 1)
                if kind == "vec":
                    ins = nc.scalar.copy(vecT[:], ps[:, 0:10])
                elif kind == "ctx":
                    ins = nc.scalar.copy(dctxT[:].rearrange("c (t g r) -> c t r g", t=TILES, r=QUADS),
                                         ps[0:D_CTX, 0:BATCH].rearrange("c (t r g) -> c t r g", t=TILES, r=QUADS))
                elif kind == "w2t":
                    ins = nc.scalar.copy(w2t[:, x0:x0 + n, :], ps[:, 0:n * H].rearrange("p (j h) -> p j h", h=H))
                elif kind == "fold":
                    ins = nc.scalar.copy(folded[:, x0:x0 + n, :],
                                         ps[:, 0:n * PAIRS].rearrange("p (j q) -> p j q", q=PAIRS))
                elif kind in ("ctA", "ctB"):
                    ins = nc.scalar.copy(ct[kind == "ctB"][:, x0:x0 + n, :, :].rearrange("p x b a -> p (x b a)"),
                                         ps[:, 0:n * HALF * HALF])
                elif kind == "wabT":
                    if x0 == 0:
                        act.wait_ge(s_pad, 1)
                    src = ps[0:HALF, 0:n * H].rearrange("p (j h) -> p j h", h=H)
                    lo = max(0, min(n, GB - x0))
                    if lo:
                        ins = nc.scalar.copy(w1c[64:64 + HALF, x0:x0 + lo, :], src[:, 0:lo, :])
                    if lo < n:
                        ins = nc.scalar.copy(w1c[96:96 + HALF, x0 + lo - GB:x0 + n - GB, :], src[:, lo:n, :])
                elif kind == "w1sT":
                    nc.scalar.copy(w1sT0[:], ps[:, 0:H])
                    ins = nc.scalar.copy(w1c[0:C1, 0, :], ps[0:C1, H:2 * H])
                elif kind == "v0":
                    ins = nc.scalar.copy(v0[:, x0:x0 + n, :], ps[:, 0:n * H].rearrange("p (j h) -> p j h", h=H))
                elif kind == "v1":
                    if x0 == 0:
                        act.wait_ge(s_pad, 1)
                    both = ps[0:C1, 0:n * H].rearrange("p (s o h) -> p s o h", o=2, h=H)
                    half = slice(x0 // 2, (x0 + n) // 2)
                    nc.scalar.copy(v1[0:C1, half, :], both[:, :, 0, :])
                    ins = nc.scalar.copy(v1[64:64 + C1, half, :], both[:, :, 1, :])
                ins.then_inc(s_sf, 1)

            def fill_diag(t):
                act.wait_ge(s_mom, t * STEPS + STEPS)
                for part, (f0, f1, col) in enumerate(PARTS):
                    act.wait_ge(s_turn[part], t + 2)
                    for r in range(QUADS):
                        q = slice(32 * r, 32 * r + 32)
                        nc.scalar.copy(diag[q, :, f0:f1, r], prod[q, :, col:col + f1 - f0]).then_inc(s_diag, 1)

            def copy_moments(t):
                for s in range(STEPS):
                    m0, m1 = MOM[s % 2]
                    n = slice(s * NSTEP, (s + 1) * NSTEP)
                    act.wait_ge(s_mom, t * STEPS + STEPS + s + 1)
                    if s == 0:
                        act.wait_ge(s_z, t + 1)

                    def view(m, p, j0, j1, step):
                        return m[0:p, :].rearrange("p (g j r) -> p j g r", g=GSTEP, r=QUADS)[:, j0:j1:step]

                    def dst(x, p0, p, js):
                        return x[p0:p0 + p, js, n].rearrange("p j (g r) -> p j g r", r=QUADS)

                    nc.scalar.copy(dst(t1, 0, C1, slice(0, HALF + 1)), view(m1, C1, 0, JW, 2))
                    nc.scalar.copy(dst(t1, 64, C1, slice(0, HALF)), view(m1, C1, 1, JW, 2)).then_inc(s_e1, 1)
                    nc.scalar.copy(dst(t0, 0, P, slice(0, JW)), view(m0, P, 0, JW, 1)).then_inc(s_e0, 1)

            def copy_z(t):
                act.wait_ge(s_z, t + 2)
                nc.scalar.copy(z[0][:], Z1[:, 0:P]).then_inc(s_zs, 1)
                nc.scalar.activation(z[1][:], Z2[:, 0:P], ACT.Identity, bias=b2x32[:, 0:1]).then_inc(s_zs, 1)

            def relu1(t):
                act.wait_ge(s_l1, t + 1)
                for m in range(MT1):
                    nc.scalar.activation(h1[:, m, :], L1[:, m * P:(m + 1) * P], ACT.Relu,
                                         bias=vecT[:, 2 + m:3 + m]).then_inc(s_h1, 1)

            def relu2(t):
                act.wait_ge(s_l2, t + 1)
                for m in range(MT2):
                    nc.scalar.activation(h2[:, m, :], L2[:, m * P:(m + 1) * P], ACT.Relu,
                                         bias=vecT[:, 6 + m:7 + m]).then_inc(s_h2, 1)

            def copy_y(t):
                act.wait_ge(s_l3, t + 1)
                nc.scalar.copy(y[0:1, bass.ds(t * P, P)].rearrange("p (r g) -> p r g", r=QUADS),
                               L1[0:1, 0:P].rearrange("p (g r) -> p r g", r=QUADS)).then_inc(s_y, 1)

            fill_diag(0)
            copy_moments(0)
            fill_diag(1)
            copy_z(0)
            with nc.scalar.Fori(1, TILES - 1) as t:
                copy_moments(t)
                relu1(t - 1)
                fill_diag(t + 1)
                relu2(t - 1)
                copy_y(t - 1)
                copy_z(t)
            copy_moments(TILES - 1)
            relu1(TILES - 2)
            relu2(TILES - 2)
            copy_y(TILES - 2)
            copy_z(TILES - 1)
            relu1(TILES - 1)
            relu2(TILES - 1)
            copy_y(TILES - 1)

        @block.vector
        def _(dve):
            chain = [0]

            def link(ins):
                chain[0] += 1
                ins.then_inc(s_dv, 1)

            def linked():
                dve.wait_ge(s_dv, chain[0])

            for part in range(3):
                dve.sem_inc(s_turn[part], 1)
            dve.wait_ge(s_w1, 16)
            nc.vector.tensor_tensor(w1ab[:], w1[:, 0:HALF, HALF:FIELDS].rearrange("h a b -> h b a"),
                                    w1[:, HALF:FIELDS, 0:HALF], ALU.add).then_inc(s_w1s, 1)
            w1f = w1[:].rearrange("h i l -> h (i l)")
            step = FIELDS + 1

            def diagonal(i, l, n):
                a = i * FIELDS + l
                return w1f[:, a:a + (n - 1) * step + 1:step]

            for side in range(2):
                o = side * HALF
                for d in range(SHIFTS):
                    c = side * HPAIR + d * HALF
                    if d == 0:
                        nc.vector.tensor_copy(w1s[:, c:c + HALF], diagonal(o, o, HALF))
                        continue
                    k = HALF - d
                    nc.vector.tensor_tensor(w1s[:, c:c + k], diagonal(o, o + d, k), diagonal(o + d, o, k), ALU.add)
                    nc.vector.tensor_tensor(w1s[:, c + k:c + HALF], diagonal(o + k, o, d), diagonal(o, o + k, d), ALU.add)
            dve.wait_ge(s_sf, where["vec", 0])
            nc.vector.tensor_scalar(b2x32[:], vecT[:, 1:2], float(EMB), None, ALU.mult)
            nc.vector.tensor_copy(w1s[:, PAIRS - 1:PAIRS], vecT[:, 0:1]).then_inc(s_w1s, 1)
            link(nc.vector.memset(w1c[:], 0.0))
            link(nc.vector.memset(v1[32:64, :, :], 0.0))
            link(nc.vector.memset(prod[:, :, PAIRS:COL_A], 0.0))
            link(nc.vector.memset(prod[:, :, PAIRS - 1], 1.0))
            link(nc.vector.memset(diag[:], 0.0))
            link(nc.vector.memset(t1[96:P, HALF + GB - 1, :], 0.0))
            link(nc.vector.memset(t1[32:64, 0:HALF + 1, :], 0.0))
            linked()
            for r in range(QUADS):
                ins = nc.vector.memset(diag[32 * r:32 * r + 32, :, ONE, r], 1.0)
            ins.then_inc(s_pad, 1)
            for side in range(2):
                dve.wait_ge(s_sf, done["ctB" if side else "ctA"])
                js = slice(HALF, FIELDS) if side == 0 else slice(0, HALF)
                for second in range(2):
                    for d in range(second, SHIFTS):
                        for i0, n, up in ((0, HALF - d, d), (HALF - d, d, d - HALF)):
                            if n == 0:
                                continue
                            c = side * HPAIR + d * HALF + i0
                            dest = folded[:, js, c:c + n]
                            term = skew(ct[side], i0, i0 + up, n) if second else skew(ct[side], i0 + up, i0, n)
                            ins = nc.vector.tensor_tensor(dest, dest, term, ALU.add)
                    if second:
                        ins.then_inc(s_cross, 1)
                    else:
                        link(ins)
                        linked()

            with nc.vector.Fori(0, TILES) as t:
                dve.wait_ge(s_mom, t * STEPS + STEPS)
                for part, (f0, f1, col) in enumerate(PARTS):
                    dve.wait_ge(s_got[part], (t + 1) * (16 * (f1 - f0)))
                    nc.vector.transpose(prod[:, :, col:col + f1 - f0].rearrange("p g f -> p f g"),
                                        rows[:, f0:f1, :]).then_inc(s_turn[part], 1)
                    if part == 0:
                        dve.wait_ge(s_turn[0], t + 2)
                        nc.vector.tensor_copy(prod[:, :, COL_A + HALF:COL_A + HALF + WRAP],
                                              prod[:, :, COL_A:COL_A + WRAP]).then_inc(s_dup, 1)
                        nc.vector.tensor_copy(prod[:, :, COL_A2:COL_A2 + HALF], prod[:, :, COL_A:COL_A + HALF])
                        dve.wait_ge(s_dup, t * 2 + 1)
                        products(nc.vector, prod, 0, GROUPS, COL_A, 0).then_inc(s_pa, 1)
                    if part == 1:
                        dve.wait_ge(s_turn[1], t + 2)
                        nc.vector.tensor_copy(prod[:, :, COL_B + HALF:COL_B + HALF + WRAP],
                                              prod[:, :, COL_B:COL_B + WRAP]).then_inc(s_dup, 1)
                dve.wait_ge(s_turn[2], t + 2)
                dve.wait_ge(s_dup, t * 2 + 2)
                for s in range(STEPS + 2):
                    if s < STEPS:
                        products(nc.vector, prod, s * GSTEP, GSTEP, COL_B, HPAIR).then_inc(s_pb, 1)
                    if s >= 2:
                        m1 = MOM[s % 2][1]
                        dve.wait_ge(s_mom, t * STEPS + STEPS + s - 1)
                        dve.wait_ge(s_e1, t * STEPS + s - 1)
                        if s == 2:
                            dve.wait_ge(s_z, t + 1)
                        n = slice((s - 2) * NSTEP, (s - 1) * NSTEP)
                        for p0, p, b0, b1_ in ((64, 32, 0, GB), (96, HALF, GB, HALF)):
                            ins = nc.vector.tensor_copy(
                                t1[p0:p0 + p, HALF:HALF + b1_ - b0, n].rearrange("p j (g r) -> p j g r", r=QUADS),
                                m1[p0:p0 + p, :].rearrange("p (g j r) -> p j g r", g=GSTEP,
                                                           r=QUADS)[:, HALF + b0:HALF + b1_])
                        ins.then_inc(s_eg, 1)


def skew(ct, x, a, n):
    return with_dims(ct[:, x, :, a:a + 1], [HALF, HALF], [HALF * HALF + 1, n])


def with_dims(ap, *dims):
    return bass.AP(tensor=ap.tensor, offset=ap.offset, ap=[list(ap.ap[0])] + [list(d) for d in dims])


def products(eng, prod, g0, groups, col, pair0):
    dst = prod[:, g0:g0 + groups, pair0:pair0 + HPAIR].rearrange("p g (d i) -> p g d i", i=HALF)
    start = prod[:, g0:g0 + groups, col:col + HALF]
    left = with_dims(start, [PCOLS, groups], [0, SHIFTS], [1, HALF])
    right = with_dims(start, [PCOLS, groups], [1, SHIFTS], [1, HALF])
    return eng.tensor_tensor(dst, left, right, ALU.mult)


NAMES = (["dense_ctx", "ids"] + [f"tbl_{i}" for i in range(FIELDS)]
         + ["W_top1", "b_top1", "W_top2", "b_top2", "W_top3", "L0_rec_W1", "L0_rec_b1", "L0_rec_W2", "L0_rec_b2"])


def kernel(**inputs):
    import numpy as _np
    import concourse.bacc as _bacc
    from concourse import mybir as _mybir
    from concourse.bass_utils import run_bass_kernel_spmd as _run

    nc = _bacc.Bacc("TRN2", target_bir_lowering=False, num_devices=1)
    arrays, aps = {}, {}
    for name in NAMES:
        a = _np.ascontiguousarray(inputs[name])
        arrays[f"in_{name}_dram"] = a
        aps[name] = nc.dram_tensor(f"in_{name}_dram", a.shape, _mybir.dt.from_np(a.dtype), kind="ExternalInput").ap()
    out = nc.dram_tensor("out_0_dram", (BATCH, 1), _mybir.dt.float32, kind="ExternalOutput").ap()
    dlrm_tower(nc, aps["dense_ctx"], aps["ids"], [aps[f"tbl_{i}"] for i in range(FIELDS)],
               aps["W_top1"], aps["b_top1"], aps["W_top2"], aps["b_top2"], aps["W_top3"],
               aps["L0_rec_W1"], aps["L0_rec_b1"], aps["L0_rec_W2"], aps["L0_rec_b2"], out)
    r = _run(nc, [arrays], core_ids=[0])
    return r.results[0]["out_0_dram"]
```

```python
from contextlib import ExitStack

import concourse.bass as bass
from concourse import mybir

F32 = mybir.dt.float32
I32 = mybir.dt.int32
ALU = mybir.AluOpType
ACT = mybir.ActivationFunctionType

P = 128
EMB = 32
FIELDS = 26
HALF = FIELDS // 2
SHIFTS = HALF // 2 + 1
WRAP = SHIFTS - 1
HPAIR = HALF * SHIFTS
PAIRS = 2 * HPAIR + 1
C1 = PAIRS - P
C, D = (0, 5), (5, 6)
JLOW = 11


def inside(group, first):
    f0, size = group
    rows = []
    for d in range(size):
        rows.append((first, f0, d, size - d))
        first += size - d
    return rows


PC = inside(C, HPAIR)
PD = inside(D, PC[-1][0] + 1)
PONE = PD[-1][0] + 1
PCD = PONE + 1
P11 = PCD + C[1] * D[1]
P12 = P11 + JLOW + 1
assert PONE == P - 1 and P12 + HALF == PAIRS
ONE = FIELDS
JW = FIELDS + 1
J1 = JW - JLOW
H = 128
BATCH = 512
TILES = BATCH // P
QUADS = 4
GROUPS = P // QUADS
GSTEP = 4
STEPS = GROUPS // GSTEP
NSTEP = GSTEP * QUADS

COL_A = P + 64
COL_B = COL_A + HALF
PCOLS = COL_B + HALF + WRAP
M1 = 64 + HALF

GRAM = J1 // 2
GSLOTS = 4
BANDS = [(64, 0, 4, 0), (96, 4, 4, 0), (0, 8, 3, 1), (32, 11, 2, 1)]
K1 = 96 + HALF

PARTS = [(0, 13, COL_A), (13, 23, COL_B), (23, 26, COL_B + 10)]

WARM = 24
D_CTX = 16
N_TOP1 = 512
N_TOP2 = 256
MT1 = N_TOP1 // P
MT2 = N_TOP2 // P


def dlrm_tower(nc, dense_ctx, ids, tables, W_top1, b_top1, W_top2, b_top2, W_top3, W1, b1, W2, b2, out):
    with ExitStack() as ctx:
        def sb(name, shape, dt=F32):
            return ctx.enter_context(nc.sbuf_tensor(name, shape, dt))

        def sem(name):
            return ctx.enter_context(nc.semaphore(name))

        w1 = sb("w1", [P, FIELDS, FIELDS])
        w2 = sb("w2", [P, H, FIELDS])
        wt1 = sb("wt1", [P, 2, N_TOP1])
        wt1c = sb("wt1c", [D_CTX, N_TOP1])
        wt2 = sb("wt2", [P, MT1, N_TOP2])
        vec = sb("vec", [10, P])
        dctx = sb("dctx", [P, TILES, D_CTX])
        ident = sb("ident", [P, P])
        ones = sb("ones", [P, P])
        vecT = sb("vecT", [P, 10])
        b2x32 = sb("b2x32", [P, 1])
        dctxT = sb("dctxT", [D_CTX, BATCH])
        w2t = sb("w2t", [P, FIELDS, H])
        w1ab = sb("w1ab", [P, HALF, HALF])
        w1s = sb("w1s", [P, PAIRS])
        ct = [sb(f"ct{s}", [P, HALF, HALF, HALF]) for s in range(2)]
        folded = sb("folded", [P, FIELDS, PAIRS])
        v0 = sb("v0", [P, FIELDS, H])
        v1 = sb("v1", [P, GRAM, H])
        w1sT0 = sb("w1sT0", [P, H])
        w1c = sb("w1c", [P, GSLOTS, H])
        idx = [sb(f"idx{i}", [P, FIELDS], I32) for i in range(2)]
        rows = sb("rows", [P, FIELDS, EMB])
        prod = sb("prod", [P, GROUPS, PCOLS])
        diag = sb("diag", [P, GROUPS, JW, QUADS])
        t0 = sb("t0", [P, JW, P])
        t1 = sb("t1", [P, GRAM + GSLOTS, P])
        z = [sb(f"z{i}", [P, P]) for i in range(2)]
        h1 = sb("h1", [P, MT1, P])
        h2 = sb("h2", [P, MT2, P])
        y = sb("y", [1, BATCH])

        bank = [ctx.enter_context(nc.psum_tensor(f"bank{i}", [P, 512], F32)) for i in range(8)]
        MOM = [(bank[0], bank[1]), (bank[2], bank[3])]
        Z1, Z2 = bank[4], bank[5]
        L1 = [bank[6], bank[7], bank[2], bank[3]]
        L2, L2_LAST = bank[6:8], bank[4:6]
        L3 = bank[6]

        s_w1, s_w2, s_vec, s_ctx, s_wt = (sem(n) for n in ("s_w1", "s_w2", "s_vec", "s_ctx", "s_wt"))
        s_idx = [sem(f"s_idx{i}") for i in range(2)]
        s_got = [sem(f"s_got{i}") for i in range(3)]
        s_ident = sem("s_ident")
        s_pad = sem("s_pad")
        s_dv = sem("s_dv")
        s_w1s = sem("s_w1s")
        s_cross = sem("s_cross")
        s_su = sem("s_su")
        s_sf = sem("s_sf")
        s_turn = [sem(f"s_turn{i}") for i in range(3)]
        s_dup = sem("s_dup")
        s_diag = sem("s_diag")
        s_pa = sem("s_pa")
        s_pb = sem("s_pb")
        s_mom = sem("s_mom")
        s_e1 = sem("s_e1")
        s_e0 = sem("s_e0")
        s_eg = sem("s_eg")
        s_z = sem("s_z")
        s_zs = sem("s_zs")
        s_l1 = sem("s_l1")
        s_h1 = sem("s_h1")
        s_l2 = sem("s_l2")
        s_h2 = sem("s_h2")
        s_l3 = sem("s_l3")
        s_y = sem("s_y")
        s_out = sem("s_out")
        s_go = sem("s_go")

        setup = [("vec", 0, 1)]
        setup += [("w2t", j, min(4, FIELDS - j)) for j in range(0, FIELDS, 4)]
        setup += [("fold", j, 2) for j in range(0, FIELDS, 2)]
        setup += [("ctA", x, min(3, HALF - x)) for x in range(0, HALF, 3)]
        setup += [("ctB", x, min(3, HALF - x)) for x in range(0, HALF, 3)]
        setup += [("ctx", 0, TILES)]
        setup += [("wabT", b, n) for _, b, n, _ in BANDS]
        setup += [("w1sT", 0, 2)]
        setup += [("v0", j, min(4, FIELDS - j)) for j in range(HALF, FIELDS, 4)]
        before = len(setup)
        setup += [("v1", x, min(4, J1 - 1 - x)) for x in range(0, J1 - 1, 4)]
        setup += [("v0", j, min(4, HALF - j)) for j in range(0, HALF, 4)]
        where = {}
        for q, (kind, first, n) in enumerate(setup):
            where[kind, first] = q + 1
        done = {kind: where[kind, first] for kind, first, n in setup}
        ring = where["w1sT", 0]
        setup_bank = [q % 6 for q in range(ring)] + [4, 5, 6, 7] * 2 + [6, 7] * 2
        assert len(setup_bank) == len(setup)

        def freed(q):
            return max([p + 1 for p in range(q) if setup_bank[p] == setup_bank[q]], default=0)

        block = ctx.enter_context(nc.Block())

        @block.sync
        def _(sp):
            ids_v = ids.rearrange("(t p) f -> t p f", p=P)
            for i in range(2):
                sp.dma_start(idx[i][:], ids_v[i]).then_inc(s_idx[i], 16)
            sp.dma_start(w1[:], W1).then_inc(s_w1, 16)
            sp.dma_start(w2[:, 0:H // 2, :], W2[:, 0:H // 2, :]).then_inc(s_w2, 16)
            sp.dma_start(wt1[:], W_top1[0:2 * H, :].rearrange("(c p) n -> p c n", p=P)).then_inc(s_wt, 16)
            sp.dma_start(wt1c[:], W_top1[2 * H:2 * H + D_CTX, :]).then_inc(s_wt, 16)
            sp.dma_start(wt2[:], W_top2.rearrange("(c p) n -> p c n", p=P)).then_inc(s_wt, 16)
            for i in range(2):
                for part, (f0, f1, _) in enumerate(PARTS):
                    sp.wait_ge(s_got[part], 16 * (f1 - f0) * (i + 1))
                sp.dma_start(idx[i][:], ids_v[2 + i]).then_inc(s_idx[i], 16)
            sp.wait_ge(s_y, 1 + TILES)
            sp.dma_start(out.rearrange("(o b) c -> o (b c)", o=1), y[:]).then_inc(s_out, 16)
            sp.wait_ge(s_out, 16)

        @block.gpsimd
        def _(pool):
            nc.gpsimd.memset(ones[:], 1.0).then_inc(s_ident, 1)
            pool.wait_ge(s_ident, 1)
            nc.gpsimd.affine_select(out=ident[:], in_=ones[:], compare_op=ALU.is_equal, fill=0.0, base=0,
                                    pattern=[[-1, P]], channel_multiplier=1).then_inc(s_ident, 1)
            with nc.gpsimd.Fori(0, TILES // 2) as u:
                for i in range(2):
                    pool.wait_ge(s_idx[i], u * 16 + 16)
                    for part, (f0, f1, _) in enumerate(PARTS):
                        pool.wait_ge(s_turn[part], u * 2 + i + 1)
                        pool.sem_inc(s_go, 1)
                        for f in range(f0, f1):
                            pool.indirect_dma_start(
                                rows[:, f, :], None, tables[f],
                                bass.IndirectOffsetOnAxis(ap=idx[i][:, f:f + 1], axis=0)).then_inc(s_got[part], 16)

        @block.tensor
        def _(pe):
            pe.sem_inc(s_mom, STEPS)
            pe.sem_inc(s_z, 2)
            pe.sem_inc(s_y, 1)
            pe.sem_inc(s_h1, MT1)
            pe.wait_ge(s_ident, 2)

            for _ in range(WARM):
                nc.tensor.matmul(bank[7][:, 0:P], ident[:], ident[:], start=True, stop=True)

            def make(q):
                kind, x0, n = setup[q]
                ps = bank[setup_bank[q]]
                if freed(q):
                    pe.wait_ge(s_sf, freed(q))
                if kind == "vec":
                    pe.wait_ge(s_vec, 80)
                    mm = nc.tensor.transpose(ps[:, 0:10], vec[:], ident[0:10, 0:10])
                elif kind == "ctx":
                    pe.wait_ge(s_ctx, 16)
                    for i in range(n):
                        mm = nc.tensor.transpose(ps[0:D_CTX, i * P:(i + 1) * P], dctx[:, i, :], ident[:])
                elif kind == "w2t":
                    if x0 == 0:
                        pe.wait_ge(s_w2, 32)
                    for i in range(n):
                        mm = nc.tensor.transpose(ps[:, i * H:(i + 1) * H], w2[:, :, x0 + i], ident[:])
                elif kind == "fold":
                    if x0 == 0:
                        pe.wait_ge(s_w1s, 2)
                        pe.wait_ge(s_sf, done["w2t"])
                    for i in range(n):
                        mm = nc.tensor.matmul(ps[:, i * PAIRS:(i + 1) * PAIRS], w2t[:, x0 + i, :], w1s[:],
                                              start=True, stop=True)
                elif kind in ("ctA", "ctB"):
                    lo = 0 if kind == "ctA" else HALF
                    rhs = w1ab[:] if kind == "ctA" else w1ab[:].rearrange("h b a -> h a b")
                    for i in range(n):
                        mm = nc.tensor.matmul(ps[:, i * HALF * HALF:(i + 1) * HALF * HALF], w2t[:, lo + x0 + i, :], rhs,
                                              start=True, stop=True)
                elif kind == "wabT":
                    for i in range(n):
                        mm = nc.tensor.transpose(ps[0:HALF, i * H:(i + 1) * H], w1ab[:, x0 + i, :], ident[:])
                elif kind == "w1sT":
                    nc.tensor.transpose(ps[:, 0:H], w1s[:, 0:P], ident[:])
                    mm = nc.tensor.transpose(ps[0:C1, H:2 * H], w1s[:, P:PAIRS], ident[:])
                elif kind == "v0":
                    if x0 in (0, HALF):
                        pe.wait_ge(s_cross, 2 if x0 else 3)
                    for i in range(n):
                        mm = nc.tensor.transpose(ps[:, i * H:(i + 1) * H], folded[:, x0 + i, 0:P], ident[:])
                elif kind == "v1":
                    for i in range(n):
                        mm = nc.tensor.transpose(ps[0:C1, i * H:(i + 1) * H], folded[:, JLOW + x0 + i, P:PAIRS], ident[:])
                mm.then_inc(s_su, 1)

            def moments(t, between=()):
                pe.wait_ge(s_diag, (t + 1) * (QUADS * len(PARTS)))
                pe.wait_ge(s_pa, t + 1)
                for s in range(STEPS):
                    m0, m1 = MOM[s % 2]
                    pe.wait_ge(s_pb, t * STEPS + s + 1)
                    if s == 1:
                        pe.wait_ge(s_h1, (t + 1) * MT1)
                    if s >= 2:
                        pe.wait_ge(s_e0, t * STEPS + s - 1)
                        pe.wait_ge(s_eg, t * STEPS + s - 1)
                    for g in range(GSTEP):
                        G = s * GSTEP + g
                        mov = diag[:, G, :, :].rearrange("p j r -> p (j r)")
                        nc.tensor.matmul(m0[:, g * P:g * P + JW * QUADS], prod[:, G, 0:P], mov, start=True, stop=True)
                        mm = nc.tensor.matmul(m1[0:M1, g * J1 * QUADS:(g + 1) * J1 * QUADS], prod[:, G, P:P + M1],
                                              mov[:, JLOW * QUADS:], start=True, stop=True)
                    mm.then_inc(s_mom, 1)
                    if s < len(between):
                        make(between[s])

            def z2_b(t):
                pe.wait_ge(s_e0, t * STEPS + STEPS)
                for j in range(HALF, FIELDS):
                    nc.tensor.matmul(Z2[:, 0:P], v0[:, j, :], t0[:, j, :], start=j == HALF, stop=False)

            def z2_second_chunk():
                for x in range(GRAM):
                    k = slice(0, C1 if x == GRAM - 1 else 64 + C1)
                    nc.tensor.matmul(Z2[:, 0:P], v1[k, x, :], t1[k, x, :], start=False, stop=False)

            def z1(t):
                nc.tensor.matmul(Z1[:, 0:P], w1sT0[:], t0[:, ONE, :], start=True, stop=False)
                pe.wait_ge(s_eg, t * STEPS + STEPS)
                for x in range(GSLOTS):
                    mm = nc.tensor.matmul(Z1[:, 0:P], w1c[0:K1, x, :], t1[0:K1, GRAM + x, :], start=False,
                                          stop=x == GSLOTS - 1)
                mm.then_inc(s_z, 1)

            def z2_a():
                for j in range(HALF):
                    mm = nc.tensor.matmul(Z2[:, 0:P], v0[:, j, :], t0[:, j, :], start=False, stop=j == HALF - 1)
                mm.then_inc(s_z, 1)

            def chunk(m):
                return slice(m * P, (m + 1) * P)

            def mlp1(t):
                pe.wait_ge(s_y, t + 1)
                for m in range(MT1):
                    nc.tensor.matmul(L1[m][:, 0:P], wt1c[:, chunk(m)], dctxT[:, bass.ds(t * P, P)], start=True, stop=False)
                for c in range(2):
                    pe.wait_ge(s_zs, t * 2 + c + 1)
                    for m in range(MT1):
                        mm = nc.tensor.matmul(L1[m][:, 0:P], wt1[:, c, chunk(m)], z[c][:], start=False, stop=c == 1)
                        if c == 1:
                            mm.then_inc(s_l1, 1)

            def mlp2(t, banks):
                for m in range(MT2):
                    for c in range(MT1):
                        if m == 0:
                            pe.wait_ge(s_h1, (t + 1) * MT1 + c + 1)
                        mm = nc.tensor.matmul(banks[m][:, 0:P], wt2[:, c, chunk(m)], h1[:, c, :], start=c == 0,
                                              stop=c == MT1 - 1)
                    mm.then_inc(s_l2, 1)

            def mlp3(t):
                for c in range(MT2):
                    pe.wait_ge(s_h2, t * MT2 + c + 1)
                    mm = nc.tensor.matmul(L3[0:1, 0:P], vecT[:, 8 + c:9 + c], h2[:, c, :], start=c == 0, stop=c == MT2 - 1)
                mm.then_inc(s_l3, 1)

            for q in range(before):
                make(q)
            pe.wait_ge(s_sf, ring)
            pe.wait_ge(s_pad, 1)
            moments(0, range(before, done["v1"]))
            for q in range(done["v1"], done["v1"] + 2):
                make(q)
            z2_b(0)
            z1(0)
            for q in range(done["v1"] + 2, len(setup)):
                make(q)
            z2_second_chunk()
            pe.wait_ge(s_sf, len(setup))
            z2_a()
            pe.wait_ge(s_wt, 48)
            mlp1(0)
            with nc.tensor.Fori(1, TILES) as t:
                moments(t)
                mlp2(t - 1, L2)
                z2_b(t)
                z1(t)
                mlp3(t - 1)
                z2_second_chunk()
                z2_a()
                mlp1(t)
            mlp2(TILES - 1, L2_LAST)
            mlp3(TILES - 1)

        @block.scalar
        def _(act):
            act.dma_start(w2[:, H // 2:H, :], W2[:, H // 2:H, :]).then_inc(s_w2, 16)
            act.dma_start(vec[0:1, :], b1.rearrange("(o n) -> o n", o=1)).then_inc(s_vec, 16)
            act.dma_start(vec[1:2, :], b2.rearrange("(o n) -> o n", o=1)).then_inc(s_vec, 16)
            act.dma_start(vec[2:6, :], b_top1.rearrange("(o n) -> o n", n=P)).then_inc(s_vec, 16)
            act.dma_start(vec[6:8, :], b_top2.rearrange("(o n) -> o n", n=P)).then_inc(s_vec, 16)
            act.dma_start(vec[8:10, :], W_top3.rearrange("(o n) c -> o (n c)", n=P)).then_inc(s_vec, 16)
            act.dma_start(dctx[:], dense_ctx.rearrange("(t p) c -> p t c", p=P)).then_inc(s_ctx, 16)

            def take(q):
                kind, x0, n = setup[q]
                ps = bank[setup_bank[q]]
                act.wait_ge(s_su, q + 1)
                if kind == "vec":
                    ins = nc.scalar.copy(vecT[:], ps[:, 0:10])
                elif kind == "ctx":
                    ins = nc.scalar.copy(dctxT[:].rearrange("c (t g r) -> c t r g", t=TILES, r=QUADS),
                                         ps[0:D_CTX, 0:BATCH].rearrange("c (t r g) -> c t r g", t=TILES, r=QUADS))
                elif kind == "w2t":
                    ins = nc.scalar.copy(w2t[:, x0:x0 + n, :], ps[:, 0:n * H].rearrange("p (j h) -> p j h", h=H))
                elif kind == "fold":
                    ins = nc.scalar.copy(folded[:, x0:x0 + n, :],
                                         ps[:, 0:n * PAIRS].rearrange("p (j q) -> p j q", q=PAIRS))
                elif kind in ("ctA", "ctB"):
                    ins = nc.scalar.copy(ct[kind == "ctB"][:, x0:x0 + n, :, :].rearrange("p x b a -> p (x b a)"),
                                         ps[:, 0:n * HALF * HALF])
                elif kind == "wabT":
                    if x0 == 0:
                        act.wait_ge(s_pad, 1)
                    band, slot = next((band, slot) for band, b, _, slot in BANDS if b == x0)
                    ins = nc.scalar.copy(w1c[band:band + HALF, slot:slot + n, :],
                                         ps[0:HALF, 0:n * H].rearrange("p (j h) -> p j h", h=H))
                elif kind == "w1sT":
                    nc.scalar.copy(w1sT0[:], ps[:, 0:H])
                    ins = nc.scalar.copy(w1c[0:C1, 0, :], ps[0:C1, H:2 * H])
                elif kind == "v0":
                    ins = nc.scalar.copy(v0[:, x0:x0 + n, :], ps[:, 0:n * H].rearrange("p (j h) -> p j h", h=H))
                elif kind == "v1":
                    if x0 == 0:
                        act.wait_ge(s_pad, 1)
                    src = ps[0:C1, 0:n * H].rearrange("p (j h) -> p j h", h=H)
                    slot = x0 // 2
                    nc.scalar.copy(v1[0:C1, slot:slot + (n + 1) // 2, :], src[:, 0:n:2, :])
                    ins = nc.scalar.copy(v1[64:64 + C1, slot:slot + n // 2, :], src[:, 1:n:2, :])
                ins.then_inc(s_sf, 1)

            def fill_diag(t, parts):
                act.wait_ge(s_mom, t * STEPS + STEPS)
                for part in parts:
                    f0, f1, col = PARTS[part]
                    act.wait_ge(s_turn[part], t + 2)
                    for r in range(QUADS):
                        q = slice(32 * r, 32 * r + 32)
                        nc.scalar.copy(diag[q, :, f0:f1, r], prod[q, :, col:col + f1 - f0]).then_inc(s_diag, 1)

            def copy_moments(t, between=()):
                for s in range(STEPS):
                    m0, m1 = MOM[s % 2]
                    n = slice(s * NSTEP, (s + 1) * NSTEP)
                    act.wait_ge(s_mom, t * STEPS + STEPS + s + 1)
                    if s == 0:
                        act.wait_ge(s_z, t * 2 + 2)

                    def view(m, p, js, width):
                        return m[0:p, 0:GSTEP * width].rearrange("p (g j r) -> p j g r", g=GSTEP, r=QUADS)[:, js]

                    def dst(x, p0, p, js):
                        return x[p0:p0 + p, js, n].rearrange("p j (g r) -> p j g r", r=QUADS)

                    w = J1 * QUADS
                    nc.scalar.copy(dst(t1, 0, C1, slice(0, GRAM)), view(m1, C1, slice(0, J1, 2), w))
                    nc.scalar.copy(dst(t1, 64, C1, slice(0, GRAM - 1)), view(m1, C1, slice(1, J1 - 1, 2), w))
                    nc.scalar.copy(dst(t1, 0, C1, slice(GRAM, GRAM + 1)),
                                   view(m1, C1, slice(J1 - 1, J1), w)).then_inc(s_e1, 1)
                    nc.scalar.copy(dst(t0, 0, P, slice(0, JW)), view(m0, P, slice(0, JW), P)).then_inc(s_e0, 1)
                    if s < len(between):
                        take(between[s])

            def copy_z1(t):
                act.wait_ge(s_z, t * 2 + 3)
                nc.scalar.copy(z[0][:], Z1[:, 0:P]).then_inc(s_zs, 1)

            def copy_z2(t):
                act.wait_ge(s_z, t * 2 + 4)
                nc.scalar.activation(z[1][:], Z2[:, 0:P], ACT.Identity, bias=b2x32[:, 0:1]).then_inc(s_zs, 1)

            def relu1(t):
                for m in range(MT1):
                    act.wait_ge(s_l1, t * MT1 + m + 1)
                    nc.scalar.activation(h1[:, m, :], L1[m][:, 0:P], ACT.Relu, bias=vecT[:, 2 + m:3 + m]).then_inc(s_h1, 1)

            def relu2(t, banks):
                for m in range(MT2):
                    act.wait_ge(s_l2, t * MT2 + m + 1)
                    nc.scalar.activation(h2[:, m, :], banks[m][:, 0:P], ACT.Relu,
                                         bias=vecT[:, 6 + m:7 + m]).then_inc(s_h2, 1)

            def copy_y(t):
                act.wait_ge(s_l3, t + 1)
                nc.scalar.copy(y[0:1, bass.ds(t * P, P)].rearrange("p (r g) -> p r g", r=QUADS),
                               L3[0:1, 0:P].rearrange("p (g r) -> p r g", r=QUADS)).then_inc(s_y, 1)

            for q in range(done["fold"]):
                take(q)
            act.wait_ge(s_pad, 1)
            fill_diag(0, [0])
            for q in range(done["fold"], ring):
                take(q)
            fill_diag(0, [1, 2])
            for q in range(ring, before):
                take(q)
            copy_moments(0, range(before, done["v1"]))
            for q in range(done["v1"], len(setup)):
                take(q)
            fill_diag(1, [0])
            copy_z1(0)
            fill_diag(1, [1])
            copy_z2(0)
            fill_diag(1, [2])
            relu1(0)
            with nc.scalar.Fori(1, TILES - 1) as t:
                copy_moments(t)
                relu2(t - 1, L2)
                copy_y(t - 1)
                fill_diag(t + 1, [0])
                copy_z1(t)
                fill_diag(t + 1, [1])
                copy_z2(t)
                fill_diag(t + 1, [2])
                relu1(t)
            copy_moments(TILES - 1)
            relu2(TILES - 2, L2)
            copy_y(TILES - 2)
            copy_z1(TILES - 1)
            copy_z2(TILES - 1)
            relu1(TILES - 1)
            relu2(TILES - 1, L2_LAST)
            copy_y(TILES - 1)

        @block.vector
        def _(dve):
            chain = [0]

            def link(ins):
                chain[0] += 1
                ins.then_inc(s_dv, 1)

            def linked():
                dve.wait_ge(s_dv, chain[0])

            for part in range(3):
                dve.sem_inc(s_turn[part], 1)
            dve.wait_ge(s_w1, 16)
            nc.vector.tensor_tensor(w1ab[:], w1[:, 0:HALF, HALF:FIELDS].rearrange("h a b -> h b a"),
                                    w1[:, HALF:FIELDS, 0:HALF], ALU.add).then_inc(s_w1s, 1)
            w1f = w1[:].rearrange("h i l -> h (i l)")
            step = FIELDS + 1

            def diagonal(i, l, n):
                a = i * FIELDS + l
                return w1f[:, a:a + (n - 1) * step + 1:step]

            for d in range(SHIFTS):
                c, k, o = d * HALF, HALF - d, HALF
                if d == 0:
                    nc.vector.tensor_copy(w1s[:, c:c + HALF], diagonal(o, o, HALF))
                    continue
                nc.vector.tensor_tensor(w1s[:, c:c + k], diagonal(o, o + d, k), diagonal(o + d, o, k), ALU.add)
                nc.vector.tensor_tensor(w1s[:, c + k:c + HALF], diagonal(o + k, o, d), diagonal(o, o + k, d), ALU.add)
            for c, o, d, n in PC + PD:
                if d == 0:
                    nc.vector.tensor_copy(w1s[:, c:c + n], diagonal(o, o, n))
                else:
                    nc.vector.tensor_tensor(w1s[:, c:c + n], diagonal(o, o + d, n), diagonal(o + d, o, n), ALU.add)
            nc.vector.tensor_tensor(w1s[:, PCD:P11].rearrange("h (c d) -> h c d", d=D[1]), w1[:, 0:D[0], D[0]:JLOW],
                                    w1[:, D[0]:JLOW, 0:D[0]].rearrange("h d c -> h c d"), ALU.add)
            for x, c in ((JLOW, P11), (JLOW + 1, P12)):
                nc.vector.tensor_tensor(w1s[:, c:c + x], w1[:, x, 0:x], w1[:, 0:x, x], ALU.add)
                nc.vector.tensor_copy(w1s[:, c + x:c + x + 1], w1[:, x, x:x + 1])
            dve.wait_ge(s_sf, where["vec", 0])
            nc.vector.tensor_scalar(b2x32[:], vecT[:, 1:2], float(EMB), None, ALU.mult)
            nc.vector.tensor_copy(w1s[:, PONE:PONE + 1], vecT[:, 0:1]).then_inc(s_w1s, 1)
            link(nc.vector.memset(w1c[:], 0.0))
            link(nc.vector.memset(v1[32:64, :, :], 0.0))
            link(nc.vector.memset(prod[:, :, PAIRS:COL_A], 0.0))
            link(nc.vector.memset(prod[:, :, PONE], 1.0))
            link(nc.vector.memset(diag[:], 0.0))
            link(nc.vector.memset(t1[:, GRAM:GRAM + GSLOTS, :], 0.0))
            link(nc.vector.memset(t1[32:64, 0:GRAM, :], 0.0))
            linked()
            for r in range(QUADS):
                ins = nc.vector.memset(diag[32 * r:32 * r + 32, :, ONE, r], 1.0)
            ins.then_inc(s_pad, 1)

            def fields_in(t, part):
                f0, f1, col = PARTS[part]
                dve.wait_ge(s_got[part], (t + 1) * (16 * (f1 - f0)))
                nc.vector.transpose(prod[:, :, col:col + f1 - f0].rearrange("p g f -> p f g"),
                                    rows[:, f0:f1, :]).then_inc(s_turn[part], 1)

            def half_a(t):
                dve.wait_ge(s_mom, t * STEPS + STEPS)
                fields_in(t, 0)
                dve.wait_ge(s_turn[0], t + 2)
                products_a(nc.vector, prod).then_inc(s_pa, 1)

            def half_b(t):
                fields_in(t, 1)
                dve.wait_ge(s_turn[1], t + 2)
                nc.vector.tensor_copy(prod[:, :, COL_B + HALF:COL_B + HALF + WRAP],
                                      prod[:, :, COL_B:COL_B + WRAP]).then_inc(s_dup, 1)
                fields_in(t, 2)

            def steps(t, between=()):
                dve.wait_ge(s_turn[2], t + 2)
                dve.wait_ge(s_dup, t + 1)
                for s in range(STEPS + 2):
                    if s < STEPS:
                        products_b(nc.vector, prod, s * GSTEP, GSTEP).then_inc(s_pb, 1)
                    if between and 2 <= s < STEPS:
                        add(*between[s - 2])
                    if s >= 2:
                        m1 = MOM[s % 2][1]
                        dve.wait_ge(s_mom, t * STEPS + STEPS + s - 1)
                        dve.wait_ge(s_e1, t * STEPS + s - 1)
                        if s == 2:
                            dve.wait_ge(s_z, t * 2 + 2)
                        n = slice((s - 2) * NSTEP, (s - 1) * NSTEP)
                        for p0, b, nb, slot in BANDS:
                            ins = nc.vector.tensor_copy(
                                t1[p0:p0 + HALF, GRAM + slot:GRAM + slot + nb, n].rearrange("p j (g r) -> p j g r", r=QUADS),
                                m1[64:64 + HALF, 0:GSTEP * J1 * QUADS].rearrange(
                                    "p (g j r) -> p j g r", g=GSTEP, r=QUADS)[:, HALF - JLOW + b:HALF - JLOW + b + nb])
                        ins.then_inc(s_eg, 1)

            def add(terms, second, last):
                if second:
                    linked()
                for dest, *term in terms:
                    if term[second] is not None:
                        ins = nc.vector.tensor_tensor(dest, dest, term[second], ALU.add)
                if last:
                    ins.then_inc(s_cross, 1)
                else:
                    link(ins)

            half_a(0)
            dve.wait_ge(s_sf, where["fold", HALF - 1])
            low = low_terms(folded)
            add(low, 0, False)
            add(low, 1, True)
            dve.wait_ge(s_sf, done["ctA"])
            cross = cross_a(folded, ct[0])
            add(cross, 0, False)
            add(cross, 1, True)
            half_b(0)
            cross = cross_b(folded, ct[1])
            dve.wait_ge(s_sf, done["ctB"])
            third = -(-len(cross) // 3)
            steps(0, [(cross[x * third:(x + 1) * third], second, second == 1 and x == 2)
                      for second in range(2) for x in range(3)])
            with nc.vector.Fori(1, TILES) as t:
                half_a(t)
                half_b(t)
                steps(t)


def with_dims(ap, *dims):
    return bass.AP(tensor=ap.tensor, offset=ap.offset, ap=[list(ap.ap[0])] + [list(d) for d in dims])


def weight(folded, j, pair, *dims):
    return with_dims(folded[:, j, pair:pair + 1], *[(dj * PAIRS + dp, n) for dj, dp, n in dims])


def low_terms(folded):
    terms = []
    nd = D[1]
    for col, o, d, n in PC:
        terms.append((weight(folded, D[0], col, (1, 0, nd), (0, 1, n)),
                      weight(folded, o + d, PCD + o * nd, (0, 1, nd), (1, nd, n)),
                      weight(folded, o, PCD + (o + d) * nd, (0, 1, nd), (1, nd, n)) if d else None))
    for col, o, d, n in PD:
        terms.append((weight(folded, 0, col, (1, 0, C[1]), (0, 1, n)),
                      weight(folded, o + d, PCD, (0, nd, C[1]), (1, 1, n)),
                      weight(folded, o, PCD + d, (0, nd, C[1]), (1, 1, n)) if d else None))
    e_src = (0, P12 - P11, 2)
    e_dst = (1, 0, 2)
    for col, o, d, n in PC + PD:
        terms.append((weight(folded, JLOW, col, e_dst, (0, 1, n)),
                      weight(folded, o + d, P11 + o, e_src, (1, 1, n)),
                      weight(folded, o, P11 + o + d, e_src, (1, 1, n)) if d else None))
    terms.append((weight(folded, JLOW, PCD, e_dst, (0, nd, C[1]), (0, 1, nd)),
                  weight(folded, D[0], P11, e_src, (0, 1, C[1]), (1, 0, nd)),
                  weight(folded, 0, P11 + D[0], e_src, (1, 0, C[1]), (0, 1, nd))))
    terms.append((weight(folded, JLOW, P11, e_dst, (0, 1, JLOW)),
                  weight(folded, 0, P11 + JLOW, e_src, (1, 0, JLOW)), None))
    terms.append((weight(folded, JLOW + 1, P12, (0, 1, JLOW)),
                  weight(folded, 0, P12 + JLOW + 1, (1, 0, JLOW)), None))
    return terms


def crossed(ct, x, a, *dims):
    return with_dims(ct[:, x, 0, a:a + 1], (HALF, HALF), *[(dx * HALF * HALF + da, n) for dx, da, n in dims])


def cross_a(folded, ct):
    def dest(col, *dims):
        return weight(folded, HALF, col, (1, 0, HALF), *dims)

    terms = []
    for col, o, d, n in PC + PD:
        terms.append((dest(col, (0, 1, n)), crossed(ct, o + d, o, (1, 1, n)),
                      crossed(ct, o, o + d, (1, 1, n)) if d else None))
    terms.append((dest(PCD, (0, D[1], C[1]), (0, 1, D[1])),
                  crossed(ct, D[0], 0, (0, 1, C[1]), (1, 0, D[1])),
                  crossed(ct, 0, D[0], (1, 0, C[1]), (0, 1, D[1]))))
    for x, col in ((JLOW, P11), (JLOW + 1, P12)):
        terms.append((dest(col, (0, 1, x + 1)), crossed(ct, x, 0, (0, 1, x + 1)), None))
        terms.append((dest(col, (0, 1, x)), None, crossed(ct, 0, x, (1, 0, x))))
    return terms


def cross_b(folded, ct):
    terms = []
    for d in range(SHIFTS):
        for i, n, up in ((0, HALF - d, d), (HALF - d, d, d - HALF)):
            if n:
                terms.append((weight(folded, 0, d * HALF + i, (1, 0, HALF), (0, 1, n)),
                              crossed(ct, i + up, i, (1, 1, n)), crossed(ct, i, i + up, (1, 1, n)) if d else None))
    return terms


def products_a(eng, prod):
    def field(f, n=1):
        return prod[:, :, COL_A + f:COL_A + f + n]

    for col, o, d, n in PC + PD:
        eng.tensor_tensor(prod[:, :, col:col + n], field(o, n), field(o + d, n), ALU.mult)
    start = field(0)
    eng.tensor_tensor(prod[:, :, PCD:P11].rearrange("p g (c d) -> p g c d", d=D[1]),
                      with_dims(start, (PCOLS, GROUPS), (1, C[1]), (0, D[1])),
                      with_dims(field(D[0]), (PCOLS, GROUPS), (0, C[1]), (1, D[1])), ALU.mult)
    for x, col in ((JLOW, P11), (JLOW + 1, P12)):
        ins = eng.tensor_tensor(prod[:, :, col:col + x + 1], field(0, x + 1),
                                with_dims(field(x), (PCOLS, GROUPS), (0, x + 1)), ALU.mult)
    return ins


def products_b(eng, prod, g0, groups):
    dst = prod[:, g0:g0 + groups, 0:HPAIR].rearrange("p g (d i) -> p g d i", i=HALF)
    start = prod[:, g0:g0 + groups, COL_B:COL_B + HALF]
    left = with_dims(start, (PCOLS, groups), (0, SHIFTS), (1, HALF))
    right = with_dims(start, (PCOLS, groups), (1, SHIFTS), (1, HALF))
    return eng.tensor_tensor(dst, left, right, ALU.mult)


NAMES = (["dense_ctx", "ids"] + [f"tbl_{i}" for i in range(FIELDS)]
         + ["W_top1", "b_top1", "W_top2", "b_top2", "W_top3", "L0_rec_W1", "L0_rec_b1", "L0_rec_W2", "L0_rec_b2"])


def kernel(**inputs):
    import numpy as _np
    import concourse.bacc as _bacc
    from concourse import mybir as _mybir
    from concourse.bass_utils import run_bass_kernel_spmd as _run

    nc = _bacc.Bacc("TRN2", target_bir_lowering=False, num_devices=1)
    arrays, aps = {}, {}
    for name in NAMES:
        a = _np.ascontiguousarray(inputs[name])
        arrays[f"in_{name}_dram"] = a
        aps[name] = nc.dram_tensor(f"in_{name}_dram", a.shape, _mybir.dt.from_np(a.dtype), kind="ExternalInput").ap()
    out = nc.dram_tensor("out_0_dram", (BATCH, 1), _mybir.dt.float32, kind="ExternalOutput").ap()
    dlrm_tower(nc, aps["dense_ctx"], aps["ids"], [aps[f"tbl_{i}"] for i in range(FIELDS)],
               aps["W_top1"], aps["b_top1"], aps["W_top2"], aps["b_top2"], aps["W_top3"],
               aps["L0_rec_W1"], aps["L0_rec_b1"], aps["L0_rec_W2"], aps["L0_rec_b2"], out)
    r = _run(nc, [arrays], core_ids=[0])
    return r.results[0]["out_0_dram"]
```
